# Optimizing a Trainium2 kernel written in Bass

```python
import numpy as np
import jax
import jax.numpy as jnp

def _softmax(x, axis=-1):
    return jax.nn.softmax(x, axis=axis)

def _gelu(x):
    return jax.nn.gelu(x, approximate=True)

def _silu(x):
    return jax.nn.silu(x)

def _sigmoid(x):
    return jax.nn.sigmoid(x)

def _layernorm(x, axis=-1, eps=1e-05):
    m = jnp.mean(x, axis=axis, keepdims=True)
    v = jnp.var(x, axis=axis, keepdims=True)
    return (x - m) / jnp.sqrt(v + eps)

def _scatter_add(tgt, idx, src, axis=0):
    return tgt.at[idx].add(src)

def _segment_sum(src, seg, n):
    return jax.ops.segment_sum(src, seg, n)
kernel_name = 'mk_adj_preln_d2_adj_r2_8ea906'

def setup_inputs(seed: int=0):
    np.random.seed(seed)
    _w = jnp.asarray

    def _rec_inputs():
        import jax
        import jax.numpy as jnp
        _gk = jax.random.key(seed)
        x = -0.0002928 + 1 * jax.random.normal(jax.random.fold_in(_gk, 1), (2048, 256), jnp.float32)
        _w = (1.0 + jnp.arange(2048, dtype=jnp.float32)) ** (-0.5)
        _w = _w / _w.mean()
        _pij = jnp.clip(0.00195312 * _w[:, None] * _w[None, :], 0.0, 1.0)
        _a = jax.random.uniform(jax.random.fold_in(_gk, 2), (2048, 2048)) < _pij
        adj = _a.astype(jnp.int32)
        return (x, adj)
    x, adj = _rec_inputs()

    def _L0_gnn_setup():
        import jax, jax.numpy as jnp
        import numpy as np
        N, D_IN, D_OUT = (4096, 256, 256)
        key = jax.random.key(seed)
        ks = jax.random.split(key, 8)
        scale_in = 1.0 / np.sqrt(D_IN)
        scale_cat = 1.0 / np.sqrt(2 * D_OUT)
        return {'x': jax.random.normal(ks[0], (N, D_IN), dtype=jnp.float32), 'adj': jax.random.randint(ks[1], (N, N), 0, 2, dtype=jnp.int32), 'W_self': jax.random.uniform(ks[2], (D_IN, D_OUT), jnp.float32, -scale_in, scale_in), 'b_self': jax.random.uniform(ks[3], (D_OUT,), jnp.float32, -scale_in, scale_in), 'W_nb': jax.random.uniform(ks[4], (D_IN, D_OUT), jnp.float32, -scale_in, scale_in), 'b_nb': jax.random.uniform(ks[5], (D_OUT,), jnp.float32, -scale_in, scale_in), 'W_comb': jax.random.uniform(ks[6], (2 * D_OUT, D_OUT), jnp.float32, -scale_cat, scale_cat), 'b_comb': jax.random.uniform(ks[7], (D_OUT,), jnp.float32, -scale_cat, scale_cat)}
    _L0_gnn_all = _L0_gnn_setup()
    _L0_gnn_in = {k: v for k, v in _L0_gnn_all.items() if k in ('W_self', 'b_self', 'W_nb', 'b_nb', 'W_comb', 'b_comb')}
    del _L0_gnn_all

    def _L1_gnn_setup():
        import jax, jax.numpy as jnp
        import numpy as np
        N = 2048
        STATE_DIM = 256
        OUTPUT_DIM = 256
        N_STEPS = 5
        W_STD = 0.02

        def _lin_params(key, out_dim, in_dim):
            W = jax.random.normal(key, (out_dim, in_dim), dtype=jnp.float32) * W_STD
            b = jnp.zeros((out_dim,), dtype=jnp.float32)
            return (W, b)
        key = jax.random.key(seed)
        ks = jax.random.split(key, 10)
        prop_state = jax.random.normal(ks[0], (N, STATE_DIM), dtype=jnp.float32)
        A = jax.random.randint(ks[1], (N, N), 0, 2, dtype=jnp.int64)
        in_W, in_b = _lin_params(ks[2], STATE_DIM, STATE_DIM)
        out_W, out_b = _lin_params(ks[3], STATE_DIM, STATE_DIM)
        r_W, r_b = _lin_params(ks[4], STATE_DIM, 3 * STATE_DIM)
        z_W, z_b = _lin_params(ks[5], STATE_DIM, 3 * STATE_DIM)
        h_W, h_b = _lin_params(ks[6], STATE_DIM, 3 * STATE_DIM)
        o1_W, o1_b = _lin_params(ks[7], STATE_DIM, STATE_DIM)
        o2_W, o2_b = _lin_params(ks[8], OUTPUT_DIM, STATE_DIM)
        return {'prop_state': prop_state, 'A': A, 'in_W': in_W, 'in_b': in_b, 'out_W': out_W, 'out_b': out_b, 'r_W': r_W, 'r_b': r_b, 'z_W': z_W, 'z_b': z_b, 'h_W': h_W, 'h_b': h_b, 'o1_W': o1_W, 'o1_b': o1_b, 'o2_W': o2_W, 'o2_b': o2_b}
    _L1_gnn_all = _L1_gnn_setup()
    _L1_gnn_in = {k: v for k, v in _L1_gnn_all.items() if k in ('in_W', 'in_b', 'out_W', 'out_b', 'r_W', 'r_b', 'z_W', 'z_b', 'h_W', 'h_b', 'o1_W', 'o1_b', 'o2_W', 'o2_b')}
    del _L1_gnn_all
    return {'x': x, 'adj': adj, 'L0_gnn_W_self': _L0_gnn_in['W_self'], 'L0_gnn_b_self': _L0_gnn_in['b_self'], 'L0_gnn_W_nb': _L0_gnn_in['W_nb'], 'L0_gnn_b_nb': _L0_gnn_in['b_nb'], 'L0_gnn_W_comb': _L0_gnn_in['W_comb'], 'L0_gnn_b_comb': _L0_gnn_in['b_comb'], 'L1_gnn_in_W': _L1_gnn_in['in_W'], 'L1_gnn_in_b': _L1_gnn_in['in_b'], 'L1_gnn_out_W': _L1_gnn_in['out_W'], 'L1_gnn_out_b': _L1_gnn_in['out_b'], 'L1_gnn_r_W': _L1_gnn_in['r_W'], 'L1_gnn_r_b': _L1_gnn_in['r_b'], 'L1_gnn_z_W': _L1_gnn_in['z_W'], 'L1_gnn_z_b': _L1_gnn_in['z_b'], 'L1_gnn_h_W': _L1_gnn_in['h_W'], 'L1_gnn_h_b': _L1_gnn_in['h_b'], 'L1_gnn_o1_W': _L1_gnn_in['o1_W'], 'L1_gnn_o1_b': _L1_gnn_in['o1_b'], 'L1_gnn_o2_W': _L1_gnn_in['o2_W'], 'L1_gnn_o2_b': _L1_gnn_in['o2_b']}

def reference(x, adj, L0_gnn_W_self, L0_gnn_b_self, L0_gnn_W_nb, L0_gnn_b_nb, L0_gnn_W_comb, L0_gnn_b_comb, L1_gnn_in_W, L1_gnn_in_b, L1_gnn_out_W, L1_gnn_out_b, L1_gnn_r_W, L1_gnn_r_b, L1_gnn_z_W, L1_gnn_z_b, L1_gnn_h_W, L1_gnn_h_b, L1_gnn_o1_W, L1_gnn_o1_b, L1_gnn_o2_W, L1_gnn_o2_b):
    import jax
    import jax.numpy as jnp

    def _L0_gnn_ref(x, adj, W_self, b_self, W_nb, b_nb, W_comb, b_comb):
        import jax, jax.numpy as jnp
        import numpy as np
        N, D_IN, D_OUT = (4096, 256, 256)
        mask = (adj > 0).astype(x.dtype)
        deg = jnp.sum(mask, axis=1, keepdims=True)
        agg = mask @ x / jnp.maximum(deg, 1.0)
        self_f = x @ W_self + b_self
        nb_f = agg @ W_nb + b_nb
        combined = jnp.concatenate([self_f, nb_f], axis=-1)
        out = combined @ W_comb + b_comb
        return jax.nn.relu(out)

    def _L1_gnn_ref(prop_state, A, in_W, in_b, out_W, out_b, r_W, r_b, z_W, z_b, h_W, h_b, o1_W, o1_b, o2_W, o2_b):
        import jax, jax.numpy as jnp
        import numpy as np
        N = 2048
        STATE_DIM = 256
        OUTPUT_DIM = 256
        N_STEPS = 5
        W_STD = 0.02

        def _lin_params(key, out_dim, in_dim):
            W = jax.random.normal(key, (out_dim, in_dim), dtype=jnp.float32) * W_STD
            b = jnp.zeros((out_dim,), dtype=jnp.float32)
            return (W, b)
        Af = A.astype(prop_state.dtype)
        AfT = Af.T
        state = prop_state
        for _ in range(N_STEPS):
            s_in = state @ in_W.T + in_b
            s_out = state @ out_W.T + out_b
            a_in = Af @ s_in
            a_out = AfT @ s_out
            a = jnp.concatenate([a_in, a_out, state], axis=-1)
            r = jax.nn.sigmoid(a @ r_W.T + r_b)
            z = jax.nn.sigmoid(a @ z_W.T + z_b)
            joined = jnp.concatenate([a_in, a_out, r * state], axis=-1)
            h_hat = jnp.tanh(joined @ h_W.T + h_b)
            state = (1.0 - z) * state + z * h_hat
        out = jnp.tanh(state @ o1_W.T + o1_b) @ o2_W.T + o2_b
        return out
    h = jnp.maximum(_layernorm(x, axis=-1), 0.0)
    x = x + _L0_gnn_ref(h, adj, L0_gnn_W_self, L0_gnn_b_self, L0_gnn_W_nb, L0_gnn_b_nb, L0_gnn_W_comb, L0_gnn_b_comb)
    h = jnp.maximum(_layernorm(x, axis=-1), 0.0)
    x = x + _L1_gnn_ref(h, adj, L1_gnn_in_W, L1_gnn_in_b, L1_gnn_out_W, L1_gnn_out_b, L1_gnn_r_W, L1_gnn_r_b, L1_gnn_z_W, L1_gnn_z_b, L1_gnn_h_W, L1_gnn_h_b, L1_gnn_o1_W, L1_gnn_o1_b, L1_gnn_o2_W, L1_gnn_o2_b)
    return x

_drawn_inputs = setup_inputs


def setup_inputs(seed=0):
    import zlib

    import numpy as np

    out = dict(_drawn_inputs(seed))
    spreads = {'L1_gnn_in_b': (0.0, 0.479),
     'L1_gnn_out_b': (0.0, 0.464),
     'L1_gnn_r_b': (0.0, 0.8),
     'L1_gnn_z_b': (0.0, 0.8),
     'L1_gnn_h_b': (0.0, 0.781),
     'L1_gnn_o1_b': (0.0, 0.1),
     'L1_gnn_o2_b': (0.0, 0.1)}
    factors = {'L0_gnn_b_self': 6.031,
     'L0_gnn_b_nb': 5.329,
     'L0_gnn_b_comb': 3.171,
     'L1_gnn_in_W': 4.72,
     'L1_gnn_out_W': 4.379,
     'L1_gnn_r_W': 8.0,
     'L1_gnn_z_W': 8.0}
    for name, (base, spread) in spreads.items():
        noise = np.random.default_rng([zlib.crc32(name.encode()), seed]).standard_normal(out[name].shape)
        drawn = base * np.exp(spread * noise) if base else spread * noise
        out[name] = jnp.asarray(drawn.astype(out[name].dtype))
    for name, factor in factors.items():
        out[name] = (out[name] * factor).astype(out[name].dtype)
    return out
```

```python
import concourse.bass as bass
from concourse import mybir
from contextlib import ExitStack

FP32 = mybir.dt.float32
FP16 = mybir.dt.float16
BF16 = mybir.dt.bfloat16
INT32 = mybir.dt.int32
ALU = mybir.AluOpType
ACT = mybir.ActivationFunctionType

P = 128
N = 2048
D = 256
NT = N // P
FT = D // P
NB = 4
BN = N // NB
BT = BN // P
GATES = 3 * D
KG = 6
STEPS = 5
SCALE = 2.0 ** 11
EPS = 1e-5
RR = 21
RING = 3
LEAD = 3
C_ID, C_ONE, C_SEL, C_MC, C_MD = 0, P, 2 * P, 2 * P + 3 * RR, 2 * P + 3 * RR + 3
C_END = C_MD + 3
STAGE_AT = [7, 12, 13]
H2_AT = 10


def graph_net(nc, x, adj, w_in, w_out, wg_t, w0_t, w_comb, w_o, cols, rows, o2_b, consts, out):
    ctx = ExitStack()
    with ctx:
        def sb(name, shape, dt):
            return ctx.enter_context(nc.sbuf_tensor(name, shape, dt))

        def sem(name):
            return ctx.enter_context(nc.semaphore(name))

        fused_d = nc.dram_tensor("fused_d", [P, 4, GATES], FP32, kind="Internal").ap()
        x1_d = nc.dram_tensor("x1_d", [P, NT, D], FP32, kind="Internal").ap()

        A = sb("A", [P, NT, N], FP16)
        AT = sb("AT", [P, NB, NT, BN], FP16)
        ST = sb("ST", [P, FT, N], FP32)
        SN = sb("SN", [P, NT, 2, D], FP16)
        work = sb("work", [P, 16384], mybir.dt.uint8)
        H = sb("H", [P, FT, BN], FP32)
        WG = sb("WG", [P, KG, GATES], FP32)
        DR = sb("DR", [P, N], BF16)
        CR = sb("CR", [P, GATES], BF16)
        cst = sb("cst", [P, C_END], FP32)
        id16 = sb("id16", [P, P], FP16)
        col = sb("col", [P, 10], FP32)
        degA = sb("degA", [P, NT, 4], FP32)
        degT = sb("degT", [P, NT, NB], FP32)
        degs = sb("degs", [P, 2, NT], FP32)
        rdeg = sb("rdeg", [P, NT], FP32)
        stat = sb("stat", [P, NT, 6], FP32)
        mv = sb("mv", [P, NT, 2], FP32)
        nrm = sb("nrm", [P, 4, NT], FP32)
        selL = sb("selL", [P, 2, RR], FP32)
        one16 = sb("one16", [P, 1], FP16)
        u_tmp = sb("u_tmp", [P, D], FP32)

        hi_lo = work[:, :].bitcast(FP16).rearrange("p (t s d) -> p t s d", t=NT, s=2)
        f32w = work[:, :].bitcast(FP32)
        PQ = f32w[:, 0:2048].rearrange("p (k n) -> p k n", k=4)
        RS = f32w[:, 2048:3072].rearrange("p (k n) -> p k n", k=2)
        Z = f32w[:, 3072:4096].rearrange("p (k n) -> p k n", k=2)
        xs = SN[:, :, :, :].rearrange("p t s d -> p t (s d)").bitcast(FP32)
        wflat = WG[:, :, :].rearrange("p k n -> p (k n)")
        ring = wflat[:, 0:RING * 1024].bitcast(INT32).rearrange("p (s r w) -> p s r w", s=RING, r=2)
        W12 = wflat[:, 3072:4096].rearrange("p (k n) -> p k n", k=4)
        bias0 = wflat[:, 4096:4352]
        mask = DR[:, :].bitcast(FP16).rearrange("p (r n) -> p r n", r=4)
        h2 = H[:, :, :].rearrange("p k n -> p (k n)").rearrange("p (q d) -> p q d", q=BT)
        Hf = H[:, :, :].rearrange("p k n -> p (k n)")
        one_col = cst[:, C_ONE:C_ONE + P]

        lateA = A[:, 8:16, :].rearrange("p t n -> p (t n)").bitcast(FP32)
        at = 0
        raw = {}
        for name, size in (("wg", 4 * GATES), ("io", 4 * D), ("w0", 4 * D), ("wc", 4 * D),
                           ("rows", GATES + D), ("Lr", 4 * RR), ("Lb", RR), ("L0", 4 * P)):
            raw[name] = lateA[:, at:at + size]
            at += size
        assert at <= 8192
        wgR = raw["wg"].rearrange("p (k n) -> p k n", k=4)
        ioR = raw["io"].rearrange("p (w j f) -> p w j f", w=2, j=2)
        w0R = raw["w0"].rearrange("p (j n) -> p j n", j=2)
        wcR = raw["wc"].rearrange("p (j n) -> p j n", j=4)
        Lr = raw["Lr"].rearrange("p (k r) -> p k r", k=4)
        L0 = raw["L0"].rearrange("p (k r) -> p k r", k=4)
        h32 = AT[:, 1, :, :].rearrange("p t n -> p (t n)").bitcast(FP32).rearrange("p (t d) -> p t d", t=NT)
        fusedS = AT[:, 3, :, :].rearrange("p t n -> p (t n)").bitcast(FP32)[:, 0:4 * GATES].rearrange(
            "p (k n) -> p k n", k=4)
        ctmp = AT[:, 2, :, :].rearrange("p t n -> p (t n)").bitcast(FP32)
        crow2 = ctmp[0:RR, 2 * GATES:2 * GATES + D]
        freeA = A[:, :, :].rearrange("p t n -> p (t n)").bitcast(FP32)
        x1o = freeA[:, 0:4096].rearrange("p (t d) -> p t d", t=NT)
        res = freeA[:, 4096:8192].rearrange("p (t d) -> p t d", t=NT)
        TT = freeA[:, 8192:10240].rearrange("p (v k n) -> p v k n", v=2, k=2)
        wo = freeA[:, 10240:11264].rearrange("p (k n) -> p k n", k=2)
        ob = freeA[:, 11264:11264 + D]

        bank = [ctx.enter_context(nc.psum_tensor(f"bank{i}", [P, 512], FP32)) for i in range(8)]
        gate_bank = bank[4:8]

        ld_x, ld_c, ld_w, ld_o = sem("ld_x"), sem("ld_c"), sem("ld_w"), sem("ld_o")
        ld_ring = [sem(f"ld_ring{i}") for i in range(RING)]
        ld_wg = sem("ld_wg")
        st_fused, st_x1, st_out = sem("st_fused"), sem("st_x1"), sem("st_out")
        id16_ready = sem("id16_ready")
        left_ready = sem("left_ready")
        fused_ready = sem("fused_ready")
        fused_out = sem("fused_out")
        w12_out = sem("w12_out")
        crow_ready, crow_out = sem("crow_ready"), sem("crow_out")
        var_ready, sqrt_ready = sem("var_ready"), sem("sqrt_ready")
        h_ready = sem("h_ready")
        h_hi, h_lo = sem("h_hi"), sem("h_lo")
        hT_ready, hT_act, hT_dve = sem("hT_ready"), sem("hT_act"), sem("hT_dve")
        conv = sem("conv")
        tr_ready = sem("tr_ready")
        at_act, at_dve = sem("at_act"), sem("at_dve")
        mask_ready, mask_used = sem("mask_ready"), sem("mask_used")
        agg_act, agg_dve = sem("agg_act"), sem("agg_dve")
        rdeg_ready = sem("rdeg_ready")
        dense_ready, x1_ready = sem("dense_ready"), sem("x1_ready")
        h2_ready, h2T_ready = sem("h2_ready"), sem("h2T_ready")
        s_act, s_dve = sem("s_act"), sem("s_dve")
        sn_hi, sn_lo = sem("sn_hi"), sem("sn_lo")
        selL_ready, drow_ready, drow_out = sem("selL_ready"), sem("drow_ready"), sem("drow_out")
        drow_used = sem("drow_used")
        agg_done = sem("agg_done")
        pq_act, pq_dve = sem("pq_act"), sem("pq_dve")
        gate_ready, gate_act = sem("gate_ready"), sem("gate_act")
        rs_ready, state_ready = sem("rs_ready"), sem("state_ready")
        turn_ready, turn_hi, turn_lo = sem("turn_ready"), sem("turn_hi"), sem("turn_lo")
        o1_ready, o1_act, o2_ready, o2_dve = sem("o1_ready"), sem("o1_act"), sem("o2_ready"), sem("o2_dve")
        dve_chain = sem("dve_chain")

        block = ctx.enter_context(nc.Block())

        @block.sync
        def _(sp):
            x_v = x.rearrange("(t p) d -> p t d", p=P)
            sp.dma_start(cst[:, :], consts).then_inc(ld_c, 16)
            sp.dma_start(col[:, :], cols).then_inc(ld_c, 16)
            sp.dma_start(xs[:, 0:8, :], x_v[:, 0:8, :]).then_inc(ld_x, 16)
            sp.dma_start(xs[:, 8:16, :], x_v[:, 8:16, :]).then_inc(ld_x, 16)
            adj_v = adj.rearrange("(b h r p) (c w) -> b c h p r w", b=NB, h=2, r=2, p=P, c=4)
            for k in range(2 * 4 * NB):
                b, c, h = k // 8, k // 2 % 4, k % 2
                if k >= RING:
                    sp.wait_ge(conv, 2 * (k - RING + 1))
                sp.dma_start(ring[:, k % RING, :, :], adj_v[b, c, h]).then_inc(ld_ring[k % RING], 16)
            sp.wait_ge(conv, 4 * NT)
            sp.wait_ge(dense_ready, NT)
            sp.wait_ge(x1_ready, NT)
            sp.wait_ge(st_fused, 16)
            sp.dma_start(WG[:, 0:4, :], fused_d).then_inc(ld_wg, 16)
            sp.dma_start(WG[:, 4:6, :], wg_t[2 * D:3 * D, :].rearrange("(k p) n -> p k n", p=P)).then_inc(ld_wg, 16)
            sp.wait_ge(agg_done, NB * STEPS)
            sp.wait_ge(st_x1, 16 * NB)
            sp.dma_start(wo, w_o.rearrange("(k p) n -> p k n", p=P)).then_inc(ld_o, 16)
            sp.dma_start(x1o, x1_d).then_inc(ld_o, 16)
            sp.dma_start(ob, o2_b.partition_broadcast(P)).then_inc(ld_o, 16)
            out_v = out.rearrange("(t p) d -> p t d", p=P)
            for b in range(NB):
                sp.wait_ge(o2_dve, 2 * (b + 1))
                sp.dma_start(out_v[:, BT * b:BT * b + BT, :], res[:, BT * b:BT * b + BT, :]).then_inc(st_out, 16)
            sp.wait_ge(st_out, 16 * NB)

        @block.gpsimd
        def _(pool):
            pool.wait_ge(fused_out, 8)
            pool.dma_start(fused_d, fusedS).then_inc(st_fused, 16)
            for b in range(NB):
                pool.wait_ge(x1_ready, BT * (b + 1))
                pool.dma_start(x1_d[:, BT * b:BT * b + BT, :], xs[:, BT * b:BT * b + BT, :]).then_inc(st_x1, 16)

        @block.tensor
        def _(pe):
            ident = cst[:, C_ID:C_ID + P]

            def mm(o, l, r, start, stop):
                return pe.matmul(o, l, r, start=start, stop=stop)

            pe.wait_ge(ld_c, 48)
            pe.wait_ge(ld_w, 16 * 5)
            for e in range(4):
                w, f = e // 2, e % 2
                if e >= 2:
                    pe.wait_ge(fused_out, 2 * (e - 1))
                for part, (lo, hi) in enumerate(((0, 512), (512, GATES))):
                    for j in range(2):
                        last = mm(bank[4 + 2 * (e % 2) + part][:, 0:hi - lo], ioR[:, w, j, f * P:f * P + P],
                                  wgR[:, 2 * w + j, lo:hi], j == 0, j == 1)
                    last.then_inc(fused_ready, 1)
            for w in range(2):
                for i in range(2):
                    for j in range(2):
                        last = mm(bank[w][:, i * D:i * D + D], w0R[:, j, w * D + i * P:w * D + i * P + P],
                                  wcR[:, 2 * w + j, :], j == 0, j == 1)
            pe.wait_ge(left_ready, 1)
            for j in range(4):
                mm(bank[2][:, 0:D], L0[:, j, :], wcR[:, j, :], j == 0, False)
            mm(bank[2][:, 0:D], cst[0:1, C_ONE:C_ONE + P], raw["rows"][0:1, GATES:GATES + D], False, True)
            for o, lo, hi in ((bank[3][0:RR, 0:512], 0, 512), (bank[2][0:RR, D:2 * D], 512, GATES)):
                for j in range(4):
                    mm(o, Lr[:, j, :], wgR[:, j, lo:hi], j == 0, False)
                last = mm(o, raw["Lb"][0:1, :], raw["rows"][0:1, lo:hi], False, True)
            last.then_inc(crow_ready, 1)
            pe.wait_ge(fused_out, 8)
            for b in range(NB):
                pe.wait_ge(h_ready, b + 1)
                if b >= 2:
                    pe.wait_ge(hT_act, b - 1)
                    pe.wait_ge(hT_dve, b - 1)
                for f in range(FT):
                    for q in range(BT):
                        last = pe.transpose(bank[4 + 2 * (b % 2) + f][:, q * P:q * P + P],
                                            h32[:, BT * b + q, f * P:f * P + P], ident)
                last.then_inc(hT_ready, 1)

            def turn_adj(i):
                b, m = i // NT, i % NT
                pe.wait_ge(conv, 4 * (4 * b + m // 4 + 1))
                if i == 0:
                    pe.wait_ge(id16_ready, 1)
                    pe.wait_ge(crow_out, 1)
                    pe.wait_ge(hT_act, NB)
                    pe.wait_ge(hT_dve, NB)
                if i >= 3:
                    if i % 2 == 1:
                        pe.wait_ge(at_act, (i - 3) // 2 + 1)
                    else:
                        pe.wait_ge(at_dve, (i - 3) // 2 + 1)
                o = bank[3 + i % 3][:, 0:256].bitcast(FP16)
                for q in range(BT):
                    last = pe.transpose(o[:, q * P:q * P + P], A[:, BT * b + q, m * P:m * P + P], id16[:, :])
                last.then_inc(tr_ready, 1)

            def mean_sum(i):
                b, m = i // NT, i % NT
                pe.wait_ge(mask_ready, i + 1)
                if m == 0 and b == 0:
                    pe.wait_ge(h_hi, 4)
                    pe.wait_ge(h_lo, 4)
                    pe.wait_ge(w12_out, 1)
                if m == 0 and b > 0:
                    pe.wait_ge(agg_act, b)
                    pe.wait_ge(agg_dve, b)
                    pe.wait_ge(rdeg_ready, b)
                mk = mask[:, i % 4, :]
                for s in range(2):
                    for f in range(FT):
                        mm(bank[f][:, :], hi_lo[:, m, s, f * P:f * P + P], mk, m == 0 and s == 0,
                           m == NT - 1 and s == 1)
                for q in range(BT):
                    last = pe.matmul(bank[2][:, BT * b + q:BT * b + q + 1], mk[:, q * P:q * P + P],
                                     one16[:, :], start=(i == 0 and q == 0), stop=(m == NT - 1),
                                     skip_group_check=True)
                last.then_inc(mask_used, 1)

            def dense(b):
                pe.wait_ge(agg_act, b + 1)
                pe.wait_ge(agg_dve, b + 1)
                if b > 0:
                    pe.wait_ge(s_act, b)
                    pe.wait_ge(s_dve, b)
                for q in range(BT):
                    if q >= 2:
                        pe.wait_ge(x1_ready, BT * b + q - 1)
                    n0 = b * BN + q * P
                    o = bank[6 + q % 2]
                    for f in range(FT):
                        mm(o[:, 0:D], ST[:, f, n0:n0 + P], W12[:, f, :], f == 0, f == 1)
                    for f in range(FT):
                        last = mm(o[:, D:2 * D], H[:, f, q * P:q * P + P], W12[:, 2 + f, :], f == 0, f == 1)
                    last.then_inc(dense_ready, 1)

            def turn_h2(b):
                pe.wait_ge(h2_ready, b + 1)
                for f in range(FT):
                    for q in range(BT):
                        last = pe.transpose(bank[6 + f][:, q * P:q * P + P], h2[:, q, f * P:f * P + P], ident)
                last.then_inc(h2T_ready, 1)

            for i in range(LEAD):
                turn_adj(i)
            for i in range(NT * NB):
                mean_sum(i)
                if i % NT == H2_AT and i > NT:
                    turn_h2(i // NT - 1)
                if i + LEAD < NT * NB:
                    turn_adj(i + LEAD)
                if i % NT == NT - 1:
                    dense(i // NT)
            turn_h2(NB - 1)

            def spread(b, m0, m1):
                for m in range(m0, m1):
                    for s in range(2):
                        for f in range(FT):
                            l = SN[:, m, s, f * P:f * P + P]
                            first, end = m == 0 and s == 0, m == NT - 1 and s == 1
                            mm(bank[f][:, :], l, AT[:, b, m, :], first, end)
                            last = mm(bank[2 + f][:, :], l, A[:, m, b * BN:b * BN + BN], first, end)
                return last

            def gates(s, b, turns):
                g = NB * s + b
                nodes = slice(b * BN, b * BN + BN)
                if b > 0:
                    pe.wait_ge(gate_act, 6 * g)
                for t in range(4):
                    o, c = gate_bank[t][:, :], t * P
                    mm(o, CR[0:RR, c:c + P], DR[0:RR, nodes], True, False)
                    for f in range(FT):
                        mm(o, WG[:, 4 + f, c:c + P], ST[:, f, nodes], False, False)
                pe.wait_ge(pq_act, 2 * (g + 1))
                pe.wait_ge(pq_dve, 2 * (g + 1))
                for t in range(6):
                    o, c = gate_bank[t % 4][:, :], t * P
                    if t == 4:
                        pe.wait_ge(gate_act, 6 * g + 2)
                    if t >= 4:
                        mm(o, CR[0:RR, c:c + P], DR[0:RR, nodes], True, False)
                    for k in range(4):
                        last = mm(o, WG[:, k, c:c + P], PQ[:, k, :], False, t < 4 and k == 3)
                    if t >= 4:
                        if t == 4:
                            pe.wait_ge(rs_ready, 2 * (g + 1))
                        for f in range(FT):
                            last = mm(o, WG[:, 4 + f, c:c + P], RS[:, f, :], False, f == 1)
                    last.then_inc(gate_ready, 1)
                    if turns and 1 <= t <= 3:
                        if t == 3:
                            pe.wait_ge(turn_hi, 8 * s + 2)
                            pe.wait_ge(turn_lo, 8 * s + 2)
                        turn_state(t - 1, (bank[0:2], bank[2:4])[(t - 1) % 2])

            def turn_state(b, banks):
                for q in range(BT):
                    for f in range(FT):
                        n0 = b * BN + q * P
                        last = pe.transpose(banks[q // 2][:, (q % 2) * D + f * P:(q % 2) * D + f * P + P],
                                            ST[:, f, n0:n0 + P], ident)
                    if q % 2 == 1:
                        last.then_inc(turn_ready, 1)

            def step(s, final):
                for b in range(NB):
                    if b > 0:
                        spread(b, 0, NT).then_inc(agg_done, 1)
                    gates(s, b, b == NB - 1 and not final)
                if final:
                    return
                pe.wait_ge(turn_hi, 8 * s + 6)
                pe.wait_ge(turn_lo, 8 * s + 6)
                spread(0, 0, NT - BT)
                pe.wait_ge(state_ready, 2 * NB * s + 2 * NB)
                turn_state(NB - 1, bank[6:8])
                pe.wait_ge(turn_hi, 8 * s + 8)
                pe.wait_ge(turn_lo, 8 * s + 8)
                spread(0, NT - BT, NT).then_inc(agg_done, 1)

            pe.wait_ge(agg_act, NB)
            pe.wait_ge(agg_dve, NB)
            pe.wait_ge(rdeg_ready, NB)
            pe.wait_ge(sn_hi, NB - 1)
            pe.wait_ge(sn_lo, NB - 1)
            pe.wait_ge(at_act, NT * NB // 2)
            pe.wait_ge(at_dve, NT * NB // 2)
            spread(0, 0, NT - BT)
            pe.wait_ge(s_act, NB)
            pe.wait_ge(s_dve, NB)
            for t in range(NT):
                pe.wait_ge(selL_ready, t + 1)
                last = mm(gate_bank[t // BT][0:RR, (t % BT) * P:(t % BT) * P + P], selL[:, t % 2, :], ident, True, True)
                last.then_inc(drow_used, 1)
            pe.wait_ge(sn_hi, NB)
            pe.wait_ge(sn_lo, NB)
            spread(0, NT - BT, NT).then_inc(agg_done, 1)
            pe.wait_ge(drow_out, NB)
            pe.wait_ge(ld_wg, 32)
            with pe.Fori(0, STEPS - 1) as s:
                step(s, False)
            step(STEPS - 1, True)

            pe.wait_ge(ld_o, 48)
            for b in range(NB):
                if b == NB - 1:
                    pe.wait_ge(state_ready, 2 * NB * STEPS)
                if b >= 2:
                    pe.wait_ge(o1_act, 2 * (b - 1))
                for o in range(2):
                    for f in range(FT):
                        last = mm(bank[2 * (b % 2) + o][:, :], wo[:, f, o * P:o * P + P],
                                  ST[:, f, b * BN:b * BN + BN], f == 0, f == 1)
                    last.then_inc(o1_ready, 1)
                pe.wait_ge(o1_act, 2 * (b + 1))
                if b == 0:
                    pe.wait_ge(gate_act, 6 * NB * STEPS)
                if b >= 2:
                    pe.wait_ge(o2_dve, 2 * (b - 1))
                for q in range(BT):
                    for o in range(2):
                        last = mm(gate_bank[2 * (b % 2) + q // 2][:, (q % 2) * D:(q % 2) * D + D],
                                  TT[:, b % 2, o, q * P:q * P + P], wo[:, o, D:2 * D], o == 0, o == 1)
                    if q % 2 == 1:
                        last.then_inc(o2_ready, 1)

        @block.scalar
        def _(act):
            def copy(o, i, scale=1.0, **kw):
                return nc.scalar.activation(o, i, ACT.Copy, scale=scale, **kw)

            act.dma_start(wgR, wg_t[0:2 * D, :].rearrange("(k p) n -> p k n", p=P)).then_inc(ld_w, 16)
            act.dma_start(ioR[:, 0], w_in.rearrange("(j p) f -> p j f", p=P)).then_inc(ld_w, 16)
            act.dma_start(ioR[:, 1], w_out.rearrange("(j p) f -> p j f", p=P)).then_inc(ld_w, 16)
            act.dma_start(w0R, w0_t.rearrange("(j p) n -> p j n", p=P)).then_inc(ld_w, 16)
            act.dma_start(wcR, w_comb.rearrange("(j p) n -> p j n", p=P)).then_inc(ld_w, 16)
            act.dma_start(raw["rows"][0:1, :], rows).then_inc(ld_c, 16)

            def convert(k, r):
                b, c, h = k // 8, k // 2 % 4, k % 2
                if r == 0:
                    act.wait_ge(ld_ring[k % RING], 16 * (k // RING + 1))
                if k == 16:
                    act.wait_ge(crow_ready, 1)
                    act.wait_ge(st_fused, 16)
                t = BT * b + 2 * h + r
                copy(A[:, t, c * 512:c * 512 + 512], ring[:, k % RING, r, :],
                     accum_out=degA[:, t, c:c + 1]).then_inc(conv, 1)

            def move_adj(i):
                b, m = i // NT, i % NT
                act.wait_ge(tr_ready, i + 1)
                if i == NT:
                    act.wait_ge(hT_ready, NB)
                    act.wait_ge(h_lo, 4)
                if i == 2 * NT:
                    act.wait_ge(crow_out, 1)
                if i == 3 * NT:
                    act.wait_ge(st_fused, 16)
                copy(AT[:, b, m, :], bank[3 + i % 3][:, 0:256].bitcast(FP16),
                     accum_out=degT[:, m, b:b + 1]).then_inc(at_act, 1)

            act.wait_ge(var_ready, 1)
            nc.scalar.activation(nrm[:, 1, :], nrm[:, 0, :], ACT.Sqrt).then_inc(sqrt_ready, 1)
            for e in range(4):
                for part, (lo, hi) in enumerate(((0, 512), (512, GATES))):
                    act.wait_ge(fused_ready, 2 * e + part + 1)
                    copy(fusedS[:, e, lo:hi], bank[4 + 2 * (e % 2) + part][:, 0:hi - lo]).then_inc(fused_out, 1)
            act.wait_ge(crow_ready, 1)
            for w in range(2):
                copy(W12[:, 2 * w:2 * w + 2, :].rearrange("p k n -> p (k n)"), bank[w][:, :])
            copy(crow2, bank[2][0:RR, D:2 * D])
            copy(bias0, bank[2][:, 0:D]).then_inc(w12_out, 1)
            for k in range(2):
                for r in range(2):
                    convert(k, r)
            for q in range(4):
                act.wait_ge(h_ready, q + 1)
                copy(hi_lo[:, BT * q:BT * q + BT, 0, :], h32[:, BT * q:BT * q + BT, :], SCALE).then_inc(h_hi, 1)
                act.wait_ge(hT_ready, q + 1)
                copy(ST[:, 0, q * BN:q * BN + BN], bank[4 + 2 * (q % 2)][:, :]).then_inc(hT_act, 1)

            def block_end(b):
                def sums():
                    act.wait_ge(mask_used, NT * (b + 1))
                    if b > 0:
                        act.wait_ge(h2T_ready, b)
                        act.wait_ge(sn_lo, b)
                    copy(H[:, 0, :], bank[0][:, :], 1.0 / SCALE).then_inc(agg_act, 1)

                def root():
                    act.wait_ge(var_ready, b + 2)
                    nc.scalar.activation(nrm[:, 1, 0:BT], nrm[:, 0, 0:BT], ACT.Sqrt).then_inc(sqrt_ready, 1)

                def state():
                    act.wait_ge(h2_ready, b + 1)
                    act.wait_ge(st_x1, 16 * (b + 1))
                    copy(SN[:, BT * b:BT * b + BT, 0, :], h2, SCALE).then_inc(sn_hi, 1)

                def turned():
                    act.wait_ge(h2T_ready, b + 1)
                    copy(ST[:, 0, b * BN:b * BN + BN], bank[6][:, :]).then_inc(s_act, 1)
                return sums, root, state, turned

            for i in range(NT * NB):
                k = 2 * (i // 4 + 1) + i % 4 // 2
                if k < 8 * NB:
                    convert(k, i % 2)
                if i % NT == 0 and i:
                    block_end(i // NT - 1)[0]()
                if i % 2 == 0:
                    move_adj(i)
                if i >= NT and i % NT in STAGE_AT:
                    block_end(i // NT - 1)[1 + STAGE_AT.index(i % NT)]()
            for stage in block_end(NB - 1):
                stage()

            def out_pq(g):
                act.wait_ge(agg_done, g + 1)
                for f in range(FT):
                    copy(PQ[:, f, :], bank[f][:, :], 1.0 / SCALE).then_inc(pq_act, 1)

            def turn(s, e, banks):
                for j in range(2):
                    act.wait_ge(turn_ready, 8 * s + e + j + 1)
                    t = 2 * (e + j)
                    copy(SN[:, t:t + 2, 0, :], banks[j][:, :].rearrange("p (t d) -> p t d", t=2),
                         SCALE).then_inc(turn_hi, 1)

            def step(s, final):
                for b in range(NB):
                    g = NB * s + b
                    out_pq(g)
                    for t in range(6):
                        act.wait_ge(gate_ready, 6 * g + t + 1)
                        if t == 2 and b > 0:
                            act.wait_ge(state_ready, 2 * g)
                        dst = (RS, Z, H)[t // 2][:, t % 2, :]
                        nc.scalar.activation(dst, gate_bank[t % 4][:, :],
                                             ACT.Tanh if t >= 4 else ACT.Sigmoid).then_inc(gate_act, 1)
                        if b == NB - 1 and not final and 1 <= t <= 3:
                            turn(s, 2 * (t - 1), (bank[0:2], bank[2:4])[(t - 1) % 2])
                if not final:
                    turn(s, 2 * (NB - 1), bank[6:8])

            with act.Fori(0, STEPS - 1) as s:
                step(s, False)
            step(STEPS - 1, True)
            for b in range(NB):
                for o in range(2):
                    act.wait_ge(o1_ready, 2 * b + o + 1)
                    if b >= 2:
                        act.wait_ge(o2_ready, 2 * (b - 1))
                    nc.scalar.activation(TT[:, b % 2, o, :], bank[2 * (b % 2) + o][:, :], ACT.Tanh,
                                         bias=col[:, 8 + o:9 + o]).then_inc(o1_act, 1)

        @block.vector
        def _(dve):
            v = nc.vector
            chain = [0]

            def link(ins):
                chain[0] += 1
                ins.then_inc(dve_chain, 1)
                dve.wait_ge(dve_chain, chain[0])

            dve.wait_ge(ld_c, 48)
            link(v.tensor_copy(id16[:, :], cst[:, C_ID:C_ID + P]))
            v.tensor_copy(one16[:, :], cst[:, C_ONE:C_ONE + 1]).then_inc(id16_ready, 1)
            for j in range(4):
                v.tensor_scalar(L0[:, j, :], one_col, col[:, 4 + j:5 + j], None, ALU.mult)
                v.tensor_scalar(Lr[:, j, :], cst[:, C_SEL + RR * (j // 2):C_SEL + RR * (j // 2 + 1)],
                                col[:, j:j + 1], None, ALU.mult)
            v.tensor_copy(raw["Lb"][0:1, :], cst[0:1, C_SEL + 2 * RR:C_SEL + 3 * RR]).then_inc(left_ready, 1)

            def stats(tiles, base):
                for t in tiles:
                    ins = v.bn_stats(stat[:, t - base, :], xs[:, t, :])
                link(ins)
                for t in tiles:
                    ins = v.bn_aggr(mv[:, t - base, :], stat[:, t - base, :])
                link(ins)
                n = len(tiles)
                v.tensor_scalar(nrm[:, 0, 0:n], mv[:, 0:n, 1], EPS, None, ALU.add).then_inc(var_ready, 1)

            def newton(n, count):
                dve.wait_ge(sqrt_ready, count)
                ve, rt, sc, rs = (nrm[:, j, 0:n] for j in range(4))
                link(v.reciprocal(sc, rt))
                link(v.tensor_tensor(sc, sc, ve, ALU.mult))
                link(v.tensor_tensor(sc, sc, rt, ALU.add))
                link(v.tensor_scalar(sc, sc, 0.5, None, ALU.mult))
                link(v.reciprocal(rs, sc))

            dve.wait_ge(ld_x, 32)
            stats(range(NT), 0)
            newton(NT, 1)
            for q in range(4):
                for t in range(BT * q, BT * q + BT):
                    ins = v.tensor_scalar(h32[:, t, :], xs[:, t, :], mv[:, t, 0:1], nrm[:, 3, t:t + 1],
                                          ALU.subtract, ALU.mult)
                link(ins)
                hq = h32[:, BT * q:BT * q + BT, :].rearrange("p t d -> p (t d)")
                v.tensor_scalar(hq, hq, 0.0, None, ALU.max).then_inc(h_ready, 1)
            for q in range(4):
                dve.wait_ge(h_hi, q + 1)
                v.scalar_tensor_tensor(out=hi_lo[:, BT * q:BT * q + BT, 1, :], in0=h32[:, BT * q:BT * q + BT, :],
                                       scalar=SCALE, in1=hi_lo[:, BT * q:BT * q + BT, 0, :],
                                       op0=ALU.mult, op1=ALU.subtract).then_inc(h_lo, 1)
                dve.wait_ge(hT_ready, q + 1)
                v.tensor_copy(ST[:, 1, q * BN:q * BN + BN], bank[5 + 2 * (q % 2)][:, :]).then_inc(hT_dve, 1)

            def split_rows(dst, srcs, tmp, masks, done):
                n = dst.shape[1]
                rest = tmp[0:RR, 0:n]
                p1 = tmp[0:RR, n:n + n // 2].bitcast(BF16)
                p2 = tmp[0:RR, n + n // 2:2 * n].bitcast(BF16)
                at = 0
                for src in srcs:
                    ins = v.tensor_copy(p1[:, at:at + src.shape[1]], src)
                    at += src.shape[1]
                link(ins)
                at = 0
                for src in srcs:
                    w = src.shape[1]
                    ins = v.tensor_tensor(rest[:, at:at + w], src, p1[:, at:at + w], ALU.subtract)
                    at += w
                if done is not None:
                    ins.then_inc(done, 1)
                    dve.wait_ge(done, 1)
                else:
                    link(ins)
                link(v.tensor_copy(p2, rest))
                m = [cst[0:RR, masks + j:masks + j + 1] for j in range(3)]
                link(v.tensor_tensor(rest, rest, p2, ALU.subtract))
                link(v.tensor_scalar(rest, rest, m[2], None, ALU.mult))
                link(v.scalar_tensor_tensor(out=rest, in0=p2, scalar=m[1], in1=rest, op0=ALU.mult, op1=ALU.add))
                return v.scalar_tensor_tensor(out=dst, in0=p1, scalar=m[0], in1=rest, op0=ALU.mult, op1=ALU.add)

            dve.wait_ge(w12_out, 1)
            split_rows(CR[0:RR, :], [bank[3][0:RR, 0:512], crow2], ctmp, C_MC,
                       None).then_inc(crow_out, 1)

            def move_adj(i):
                b, m = i // NT, i % NT
                dve.wait_ge(tr_ready, i + 1)
                if i == 3 * NT + 1:
                    dve.wait_ge(st_fused, 16)
                v.tensor_scalar(AT[:, b, m, :], bank[3 + i % 3][:, 0:256].bitcast(FP16), 1.0, None, ALU.mult,
                                ALU.add, accum_out=degT[:, m, b:b + 1]).then_inc(at_dve, 1)

            def make_mask(i):
                b, m = i // NT, i % NT
                if i % 2 == 0:
                    dve.wait_ge(at_act, i // 2 + 1)
                else:
                    dve.wait_ge(at_dve, i // 2 + 1)
                if i >= 4:
                    dve.wait_ge(mask_used, i - 3)
                v.tensor_scalar(mask[:, i % 4, :], AT[:, b, m, :], 0.0, None, ALU.is_gt).then_inc(mask_ready, 1)

            def sums(b):
                dve.wait_ge(mask_used, NT * (b + 1))
                if b > 0:
                    dve.wait_ge(h2T_ready, b)
                    dve.wait_ge(sn_hi, b)
                v.tensor_scalar(H[:, 1, :], bank[1][:, :], 1.0 / SCALE, None, ALU.mult).then_inc(agg_dve, 1)
                tiles = slice(BT * b, BT * b + BT)
                v.tensor_scalar(rdeg[:, tiles], bank[2][:, tiles], 1.0, None, ALU.max).then_inc(rdeg_ready, 1)
                dve.wait_ge(rdeg_ready, b + 1)
                link(v.reciprocal(rdeg[:, tiles], rdeg[:, tiles]))

            def residual(b):
                for q in range(BT):
                    t = BT * b + q
                    o = bank[6 + q % 2]
                    u = u_tmp[:, :]
                    dve.wait_ge(dense_ready, t + 1)
                    link(v.scalar_tensor_tensor(out=u, in0=o[:, D:2 * D], scalar=rdeg[:, t:t + 1], in1=bias0,
                                                op0=ALU.mult, op1=ALU.add))
                    link(v.tensor_tensor(u, u, o[:, 0:D], ALU.add))
                    v.scalar_tensor_tensor(out=xs[:, t, :], in0=u, scalar=0.0, in1=xs[:, t, :],
                                           op0=ALU.max, op1=ALU.add).then_inc(x1_ready, 1)
                    dve.wait_ge(x1_ready, t + 1)

            def normed(b):
                newton(BT, b + 2)
                dve.wait_ge(dense_ready, BT * (b + 1))
                for q in range(BT):
                    ins = v.tensor_scalar(h2[:, q, :], xs[:, BT * b + q, :], mv[:, q, 0:1], nrm[:, 3, q:q + 1],
                                          ALU.subtract, ALU.mult)
                link(ins)
                v.tensor_scalar(Hf, Hf, 0.0, None, ALU.max).then_inc(h2_ready, 1)

            def state(b):
                dve.wait_ge(sn_hi, b + 1)
                tiles = slice(BT * b, BT * b + BT)
                v.scalar_tensor_tensor(out=SN[:, tiles, 1, :], in0=h2, scalar=SCALE, in1=SN[:, tiles, 0, :],
                                       op0=ALU.mult, op1=ALU.subtract).then_inc(sn_lo, 1)

            def turned(b):
                dve.wait_ge(h2T_ready, b + 1)
                v.tensor_copy(ST[:, 1, b * BN:b * BN + BN], bank[7][:, :]).then_inc(s_dve, 1)

            for i in range(NT * NB + 1):
                if i:
                    make_mask(i - 1)
                if i % NT == 0 and i:
                    sums(i // NT - 1)
                if i % 2 == 1:
                    move_adj(i)
                if i % NT == 2 and i > NT or i == NT * NB:
                    residual((i - 1) // NT - (i < NT * NB))
                    b = (i - 1) // NT - (i < NT * NB)
                    stats(range(BT * b, BT * b + BT), BT * b)
                if i > NT and i % NT == STAGE_AT[0] + 1:
                    normed(i // NT - 1)
                if i > NT and i % NT == STAGE_AT[1] + 1:
                    state(i // NT - 1)
                if i > NT and i % NT == STAGE_AT[2] + 1:
                    turned(i // NT - 1)
            normed(NB - 1)
            state(NB - 1)
            turned(NB - 1)

            dve.wait_ge(conv, 4 * NT)
            dve.wait_ge(at_act, NT * NB // 2)
            v.tensor_reduce(degs[:, 0, :], degA[:, :, :], mybir.AxisListType.X, ALU.add)
            link(v.tensor_reduce(degs[:, 1, :], degT[:, :, :], mybir.AxisListType.X, ALU.add))
            sel = [cst[:, C_SEL + RR * j:C_SEL + RR * (j + 1)] for j in range(3)]
            for t in range(NT):
                if t >= 2:
                    dve.wait_ge(drow_used, t - 1)
                o = selL[:, t % 2, :]
                link(v.scalar_tensor_tensor(out=o, in0=sel[0], scalar=degs[:, 0, t:t + 1], in1=sel[2],
                                            op0=ALU.mult, op1=ALU.add))
                v.scalar_tensor_tensor(out=o, in0=sel[1], scalar=degs[:, 1, t:t + 1], in1=o,
                                       op0=ALU.mult, op1=ALU.add).then_inc(selL_ready, 1)
            dve.wait_ge(mask_used, NT * NB)
            for b in range(NB):
                dve.wait_ge(drow_used, BT * (b + 1))
                split_rows(DR[0:RR, b * BN:b * BN + BN], [gate_bank[b][0:RR, :]], Hf, C_MD,
                           None).then_inc(drow_out, 1)
                if b < NB - 1:
                    dve.wait_ge(drow_out, b + 1)

            def out_pq(g):
                dve.wait_ge(agg_done, g + 1)
                for f in range(FT):
                    v.tensor_scalar(PQ[:, 2 + f, :], bank[2 + f][:, :], 1.0 / SCALE, None,
                                    ALU.mult).then_inc(pq_dve, 1)

            def turn(s, e, banks):
                for j in range(2):
                    dve.wait_ge(turn_hi, 8 * s + e + j + 1)
                    t = 2 * (e + j)
                    v.scalar_tensor_tensor(out=SN[:, t:t + 2, 1, :],
                                           in0=banks[j][:, :].rearrange("p (t d) -> p t d", t=2),
                                           scalar=SCALE, in1=SN[:, t:t + 2, 0, :],
                                           op0=ALU.mult, op1=ALU.subtract).then_inc(turn_lo, 1)

            base = chain[0]
            PER_BLOCK = 4

            def step(s, final):
                for b in range(NB):
                    g = NB * s + b
                    nodes = slice(b * BN, b * BN + BN)
                    out_pq(g)
                    for f in range(FT):
                        dve.wait_ge(gate_act, 6 * g + f + 1)
                        v.tensor_tensor(RS[:, f, :], RS[:, f, :], ST[:, f, nodes], ALU.mult).then_inc(rs_ready, 1)
                    if b == NB - 1 and not final:
                        for e in range(3):
                            turn(s, 2 * e, (bank[0:2], bank[2:4])[e % 2])
                    for f in range(FT):
                        c = base + PER_BLOCK * g + 2 * f
                        dve.wait_ge(gate_act, 6 * g + 5 + f)
                        v.tensor_tensor(H[:, f, :], H[:, f, :], ST[:, f, nodes],
                                        ALU.subtract).then_inc(dve_chain, 1)
                        dve.wait_ge(dve_chain, c + 1)
                        v.tensor_tensor(H[:, f, :], H[:, f, :], Z[:, f, :], ALU.mult).then_inc(dve_chain, 1)
                        dve.wait_ge(dve_chain, c + 2)
                        v.tensor_tensor(ST[:, f, nodes], ST[:, f, nodes], H[:, f, :],
                                        ALU.add).then_inc(state_ready, 1)
                if not final:
                    turn(s, 2 * (NB - 1), bank[6:8])

            with dve.Fori(0, STEPS - 1) as s:
                step(s, False)
            step(STEPS - 1, True)
            dve.wait_ge(ld_o, 48)
            for t in range(NT):
                ins = v.tensor_tensor(x1o[:, t, :], x1o[:, t, :], ob, ALU.add)
            ins.then_inc(dve_chain, 1)
            dve.wait_ge(dve_chain, base + PER_BLOCK * NB * STEPS + 1)
            for e in range(2 * NB):
                dve.wait_ge(o2_ready, e + 1)
                tiles = slice(2 * e, 2 * e + 2)
                v.tensor_tensor(res[:, tiles, :].rearrange("p t d -> p (t d)"),
                                gate_bank[e % 4][:, :],
                                x1o[:, tiles, :].rearrange("p t d -> p (t d)"), ALU.add).then_inc(o2_dve, 1)


def kernel(**inputs):
    import numpy as np
    import concourse.bacc as bacc
    from concourse.bass_utils import run_bass_kernel_spmd

    a = {k: np.asarray(v) for k, v in inputs.items()}
    f = np.float32
    consts = np.zeros((P, C_END), f)
    consts[:, C_ID:C_ID + P] = np.eye(P, dtype=f)
    consts[:, C_ONE:C_ONE + P] = 1.0
    for j, (lo, hi) in enumerate(((0, 9), (9, 18), (18, RR))):
        consts[:, C_SEL + RR * j + lo:C_SEL + RR * j + hi] = 1.0
    for k in range(RR):
        consts[k, C_MC + k % 3] = 1.0
        consts[k, C_MD + (k % 9 // 3 if k < 18 else 0)] = 1.0
    two = lambda v: v.reshape(2, P).T
    arrays = {
        "x": a["x"], "adj": a["adj"],
        "w_in": a["L1_gnn_in_W"], "w_out": a["L1_gnn_out_W"],
        "wg_t": np.concatenate([a["L1_gnn_r_W"].T, a["L1_gnn_z_W"].T, a["L1_gnn_h_W"].T], 1),
        "w0_t": np.concatenate([a["L0_gnn_W_self"].T, a["L0_gnn_W_nb"].T], 1),
        "w_comb": a["L0_gnn_W_comb"],
        "w_o": np.concatenate([a["L1_gnn_o1_W"].T, a["L1_gnn_o2_W"].T], 1),
        "cols": np.concatenate([two(a["L1_gnn_in_b"]), two(a["L1_gnn_out_b"]), two(a["L0_gnn_b_self"]),
                                two(a["L0_gnn_b_nb"]), two(a["L1_gnn_o1_b"])], 1),
        "rows": np.concatenate([a["L1_gnn_r_b"], a["L1_gnn_z_b"], a["L1_gnn_h_b"], a["L0_gnn_b_comb"]])[None],
        "o2_b": a["L1_gnn_o2_b"],
        "consts": consts,
    }
    arrays = {k: np.ascontiguousarray(v) for k, v in arrays.items()}
    nc = bacc.Bacc("TRN2", target_bir_lowering=False, num_devices=1)
    args = [nc.dram_tensor(f"in_{k}", v.shape, mybir.dt.from_np(v.dtype), kind="ExternalInput").ap()
            for k, v in arrays.items()]
    out = nc.dram_tensor("out", (N, D), FP32, kind="ExternalOutput").ap()
    graph_net(nc, *args, out)
    r = run_bass_kernel_spmd(nc, [{f"in_{k}": v for k, v in arrays.items()}], core_ids=[0])
    return r.results[0]["out"]
```

```python
import concourse.bass as bass
from concourse import mybir
from contextlib import ExitStack

FP32 = mybir.dt.float32
FP16 = mybir.dt.float16
BF16 = mybir.dt.bfloat16
INT32 = mybir.dt.int32
ALU = mybir.AluOpType
ACT = mybir.ActivationFunctionType

P = 128
N = 2048
D = 256
NT = N // P
FT = D // P
NB = 4
BN = N // NB
BT = BN // P
GATES = 3 * D
KG = 6
STEPS = 5
SCALE = 2.0 ** 11
EPS = 1e-5
RR = 21
RING = 3
LEAD = 3
C_ID, C_ONE, C_SEL, C_KC, C_KD = 0, P, 2 * P, 2 * P + 3 * RR, 2 * P + 3 * RR + 2
C_END = C_KD + 2
STAGE_AT = [7, 12, 13]
H2_BANKS = [6, 6, 6, 4]
H2_AT = 10


def graph_net(nc, x, adj, w_in, w_out, wg_t, w0_t, w_comb, w_o, cols, rows, o2_b, consts, out):
    ctx = ExitStack()
    with ctx:
        def sb(name, shape, dt):
            return ctx.enter_context(nc.sbuf_tensor(name, shape, dt))

        def sem(name):
            return ctx.enter_context(nc.semaphore(name))

        fused_d = nc.dram_tensor("fused_d", [P, 4, GATES], FP32, kind="Internal").ap()
        x1_d = nc.dram_tensor("x1_d", [P, NT, D], FP32, kind="Internal").ap()

        A = sb("A", [P, NT, N], FP16)
        AT = sb("AT", [P, NB, NT, BN], FP16)
        ST = sb("ST", [P, FT, N], FP32)
        SN = sb("SN", [P, NT, 2, D], FP16)
        work = sb("work", [P, 16384], mybir.dt.uint8)
        H = sb("H", [P, FT, BN], FP32)
        WG = sb("WG", [P, KG, GATES], FP32)
        DR = sb("DR", [P, N], BF16)
        CR = sb("CR", [P, GATES], BF16)
        cst = sb("cst", [P, C_END], FP32)
        id16 = sb("id16", [P, P], FP16)
        col = sb("col", [P, 10], FP32)
        degA = sb("degA", [P, NT, 4], FP32)
        degT = sb("degT", [P, NT, NB], FP32)
        degs = sb("degs", [P, 2, NT], FP32)
        rdeg = sb("rdeg", [P, NT], FP32)
        stat = sb("stat", [P, NT, 6], FP32)
        mv = sb("mv", [P, NT, 2], FP32)
        nrm = sb("nrm", [P, 4, NT], FP32)
        one16 = sb("one16", [P, 1], FP16)

        hi_lo = work[:, :].bitcast(FP16).rearrange("p (t s d) -> p t s d", t=NT, s=2)
        f32w = work[:, :].bitcast(FP32)
        PQ = f32w[:, 0:2048].rearrange("p (k n) -> p k n", k=4)
        RS = f32w[:, 2048:3072].rearrange("p (k n) -> p k n", k=2)
        selL = f32w[:, 2048:2048 + NT * RR].rearrange("p (t r) -> p t r", t=NT)
        Z = f32w[:, 3072:4096].rearrange("p (k n) -> p k n", k=2)
        xs = SN[:, :, :, :].rearrange("p t s d -> p t (s d)").bitcast(FP32)
        wflat = WG[:, :, :].rearrange("p k n -> p (k n)")
        ring = wflat[:, 0:RING * 1024].bitcast(INT32).rearrange("p (s r w) -> p s r w", s=RING, r=2)
        W12 = wflat[:, 3072:4096].rearrange("p (k n) -> p k n", k=4)
        bias0 = wflat[:, 4096:4096 + D]
        u_tmp = wflat[:, 4096 + D:4096 + 2 * D]
        mask = DR[:, :].bitcast(FP16).rearrange("p (r n) -> p r n", r=4)
        h2 = H[:, :, :].rearrange("p k n -> p (k n)").rearrange("p (q d) -> p q d", q=BT)
        Hf = H[:, :, :].rearrange("p k n -> p (k n)")
        one_col = cst[:, C_ONE:C_ONE + P]

        lateA = A[:, 8:16, :].rearrange("p t n -> p (t n)").bitcast(FP32)
        at = 0
        raw = {}
        for name, size in (("wg", 4 * GATES), ("io", 4 * D), ("w0", 4 * D), ("wc", 4 * D),
                           ("rows", GATES + D), ("Lr", 4 * RR), ("Lb", RR), ("L0", 4 * P)):
            raw[name] = lateA[:, at:at + size]
            at += size
        assert at <= 8192
        wgR = raw["wg"].rearrange("p (k n) -> p k n", k=4)
        ioR = raw["io"].rearrange("p (w j f) -> p w j f", w=2, j=2)
        w0R = raw["w0"].rearrange("p (j n) -> p j n", j=2)
        wcR = raw["wc"].rearrange("p (j n) -> p j n", j=4)
        Lr = raw["Lr"].rearrange("p (k r) -> p k r", k=4)
        L0 = raw["L0"].rearrange("p (k r) -> p k r", k=4)
        h32 = AT[:, 1, :, :].rearrange("p t n -> p (t n)").bitcast(FP32).rearrange("p (t d) -> p t d", t=NT)
        fusedS = AT[:, 3, :, :].rearrange("p t n -> p (t n)").bitcast(FP32)[:, 0:4 * GATES].rearrange(
            "p (k n) -> p k n", k=4)
        ctmp = AT[:, 2, :, :].rearrange("p t n -> p (t n)").bitcast(FP32)
        crow = ctmp[0:RR, 2 * GATES:3 * GATES]
        freeA = A[:, :, :].rearrange("p t n -> p (t n)").bitcast(FP32)
        x1o = freeA[:, 0:4096].rearrange("p (t d) -> p t d", t=NT)
        res = freeA[:, 4096:8192].rearrange("p (t d) -> p t d", t=NT)
        TT = freeA[:, 8192:10240].rearrange("p (v k n) -> p v k n", v=2, k=2)
        wo = freeA[:, 10240:11264].rearrange("p (k n) -> p k n", k=2)
        ob = freeA[:, 11264:11264 + D]

        bank = [ctx.enter_context(nc.psum_tensor(f"bank{i}", [P, 512], FP32)) for i in range(8)]
        gate_bank = bank[4:8]

        ld_c, ld_w0, ld_o = sem("ld_c"), sem("ld_w0"), sem("ld_o")
        ld_w = [sem(f"ld_w_{w}") for w in ("in", "out")]
        ld_x = [sem(f"ld_x{i}") for i in range(2)]
        ld_ring = [sem(f"ld_ring{i}") for i in range(RING)]
        ld_wg = sem("ld_wg")
        st_fused, st_x1, st_out = sem("st_fused"), sem("st_x1"), sem("st_out")
        id16_ready = sem("id16_ready")
        left_ready = sem("left_ready")
        fused_ready = sem("fused_ready")
        fused_out = sem("fused_out")
        w12_out = sem("w12_out")
        crow_ready, crow_out = sem("crow_ready"), sem("crow_out")
        var_ready, sqrt_ready = sem("var_ready"), sem("sqrt_ready")
        h_ready = sem("h_ready")
        h_hi, h_lo = sem("h_hi"), sem("h_lo")
        hT_ready, hT_act, hT_dve = sem("hT_ready"), sem("hT_act"), sem("hT_dve")
        conv = sem("conv")
        tr_ready = sem("tr_ready")
        at_act, at_dve = sem("at_act"), sem("at_dve")
        mask_ready, mask_used = sem("mask_ready"), sem("mask_used")
        agg_act, agg_dve = sem("agg_act"), sem("agg_dve")
        rdeg_ready = sem("rdeg_ready")
        dense_ready, x1_ready = sem("dense_ready"), sem("x1_ready")
        h2_ready, h2T_ready = sem("h2_ready"), sem("h2T_ready")
        s_act, s_dve = sem("s_act"), sem("s_dve")
        sn_hi, sn_lo = sem("sn_hi"), sem("sn_lo")
        selL_ready, drow_ready, drow_out = sem("selL_ready"), sem("drow_ready"), sem("drow_out")
        ld_rows = sem("ld_rows")
        agg_done = sem("agg_done")
        pq_act, pq_dve = sem("pq_act"), sem("pq_dve")
        gate_ready, gate_act = sem("gate_ready"), sem("gate_act")
        rs_ready, state_ready = sem("rs_ready"), sem("state_ready")
        turn_ready, turn_hi, turn_lo = sem("turn_ready"), sem("turn_hi"), sem("turn_lo")
        o1_ready, o1_act, o2_ready, o2_dve = sem("o1_ready"), sem("o1_act"), sem("o2_ready"), sem("o2_dve")
        dve_chain = sem("dve_chain")

        block = ctx.enter_context(nc.Block())

        @block.sync
        def _(sp):
            x_v = x.rearrange("(t p) d -> p t d", p=P)
            for w, w_half in enumerate((w_in, w_out)):
                sp.dma_start(ioR[:, w], w_half.rearrange("(j p) f -> p j f", p=P)).then_inc(ld_w[w], 16)
                sp.dma_start(wgR[:, 2 * w:2 * w + 2, :],
                             wg_t[w * D:w * D + D, :].rearrange("(k p) n -> p k n", p=P)).then_inc(ld_w[w], 16)
            for h in range(2):
                sp.dma_start(xs[:, 8 * h:8 * h + 8, :], x_v[:, 8 * h:8 * h + 8, :]).then_inc(ld_x[h], 16)
            sp.dma_start(w0R, w0_t.rearrange("(j p) n -> p j n", p=P)).then_inc(ld_w0, 16)
            sp.dma_start(wcR, w_comb.rearrange("(j p) n -> p j n", p=P)).then_inc(ld_w0, 16)
            adj_v = adj.rearrange("(b h r p) (c w) -> b c h p r w", b=NB, h=2, r=2, p=P, c=4)
            for k in range(2 * 4 * NB):
                b, c, h = k // 8, k // 2 % 4, k % 2
                if k >= RING:
                    sp.wait_ge(conv, 2 * (k - RING + 1))
                sp.dma_start(ring[:, k % RING, :, :], adj_v[b, c, h]).then_inc(ld_ring[k % RING], 16)
            sp.wait_ge(conv, 4 * NT)
            sp.wait_ge(dense_ready, NT)
            sp.wait_ge(st_x1, 16 * NB)
            sp.wait_ge(st_fused, 16)
            sp.dma_start(WG[:, 0:4, :], fused_d).then_inc(ld_wg, 16)
            sp.dma_start(WG[:, 4:6, :], wg_t[2 * D:3 * D, :].rearrange("(k p) n -> p k n", p=P)).then_inc(ld_wg, 16)
            sp.wait_ge(agg_done, NB * STEPS)
            sp.dma_start(wo, w_o.rearrange("(k p) n -> p k n", p=P)).then_inc(ld_o, 16)
            sp.dma_start(x1o, x1_d).then_inc(ld_o, 16)
            sp.dma_start(ob, o2_b.partition_broadcast(P)).then_inc(ld_o, 16)
            out_v = out.rearrange("(t p) d -> p t d", p=P)
            for b in range(NB):
                sp.wait_ge(o2_dve, 2 * (b + 1))
                sp.dma_start(out_v[:, BT * b:BT * b + BT, :], res[:, BT * b:BT * b + BT, :]).then_inc(st_out, 16)
            sp.wait_ge(st_out, 16 * NB)

        @block.gpsimd
        def _(pool):
            pool.wait_ge(fused_out, 8)
            pool.dma_start(fused_d, fusedS).then_inc(st_fused, 16)
            for b in range(NB):
                pool.wait_ge(x1_ready, BT * (b + 1))
                pool.dma_start(x1_d[:, BT * b:BT * b + BT, :], xs[:, BT * b:BT * b + BT, :]).then_inc(st_x1, 16)
            pool.wait_ge(crow_out, 1)
            for r in range(1, 4):
                pool.dma_start(CR[32 * r:32 * r + RR, :], CR[0:RR, :]).then_inc(ld_rows, 16)
            pool.wait_ge(drow_out, NB)
            for r in range(1, 4):
                pool.dma_start(DR[32 * r:32 * r + RR, :], DR[0:RR, :]).then_inc(ld_rows, 16)

        @block.tensor
        def _(pe):
            ident = cst[:, C_ID:C_ID + P]

            def mm(o, l, r, start, stop):
                return pe.matmul(o, l, r, start=start, stop=stop)

            for e in range(4):
                w, f = e // 2, e % 2
                if f == 0:
                    pe.wait_ge(ld_w[w], 32)
                if e >= 2:
                    pe.wait_ge(fused_out, 2 * (e - 1))
                for part, (lo, hi) in enumerate(((0, 512), (512, GATES))):
                    for j in range(2):
                        last = mm(bank[4 + 2 * (e % 2) + part][:, 0:hi - lo], ioR[:, w, j, f * P:f * P + P],
                                  wgR[:, 2 * w + j, lo:hi], j == 0, j == 1)
                    last.then_inc(fused_ready, 1)
            def turn_h(b):
                pe.wait_ge(h_ready, b + 1)
                if b < 2:
                    pe.wait_ge(fused_out, 2 * b + 6)
                else:
                    pe.wait_ge(hT_act, b - 1)
                    pe.wait_ge(hT_dve, b - 1)
                for f in range(FT):
                    for q in range(BT):
                        last = pe.transpose(bank[4 + 2 * (b % 2) + f][:, q * P:q * P + P],
                                            h32[:, BT * b + q, f * P:f * P + P], ident)
                last.then_inc(hT_ready, 1)

            pe.wait_ge(ld_c, 48)
            pe.wait_ge(ld_w0, 32)
            for w in range(2):
                for i in range(2):
                    for j in range(2):
                        last = mm(bank[w][:, i * D:i * D + D], w0R[:, j, w * D + i * P:w * D + i * P + P],
                                  wcR[:, 2 * w + j, :], j == 0, j == 1)
            pe.wait_ge(left_ready, 1)
            for j in range(4):
                mm(bank[2][:, 0:D], L0[:, j, :], wcR[:, j, :], j == 0, False)
            mm(bank[2][:, 0:D], cst[0:1, C_ONE:C_ONE + P], raw["rows"][0:1, GATES:GATES + D], False, True)
            for o, lo, hi in ((bank[3][0:RR, 0:512], 0, 512), (bank[2][0:RR, D:2 * D], 512, GATES)):
                for j in range(4):
                    mm(o, Lr[:, j, :], wgR[:, j, lo:hi], j == 0, False)
                last = mm(o, raw["Lb"][0:1, :], raw["rows"][0:1, lo:hi], False, True)
            last.then_inc(crow_ready, 1)
            for b in range(NB):
                turn_h(b)

            def turn_adj(i):
                b, m = i // NT, i % NT
                pe.wait_ge(conv, 4 * (4 * b + m // 4 + 1))
                if i == 2:
                    pe.wait_ge(w12_out, 1)
                if i == 0:
                    pe.wait_ge(id16_ready, 1)
                    pe.wait_ge(hT_act, NB)
                    pe.wait_ge(hT_dve, NB)
                if i >= 3:
                    if i % 2 == 1:
                        pe.wait_ge(at_act, (i - 3) // 2 + 1)
                    else:
                        pe.wait_ge(at_dve, (i - 3) // 2 + 1)
                o = bank[3 + (i + 1) % 3][:, 0:256].bitcast(FP16)
                for q in range(BT):
                    last = pe.transpose(o[:, q * P:q * P + P], A[:, BT * b + q, m * P:m * P + P], id16[:, :])
                last.then_inc(tr_ready, 1)

            def mean_sum(i):
                b, m = i // NT, i % NT
                pe.wait_ge(mask_ready, i + 1)
                if m == 0 and b == 0:
                    pe.wait_ge(h_hi, 4)
                    pe.wait_ge(h_lo, 4)
                    pe.wait_ge(w12_out, 1)
                if m == 0 and b > 0:
                    pe.wait_ge(agg_act, b)
                    pe.wait_ge(agg_dve, b)
                    pe.wait_ge(rdeg_ready, b)
                mk = mask[:, i % 4, :]
                for s in range(2):
                    for f in range(FT):
                        mm(bank[f][:, :], hi_lo[:, m, s, f * P:f * P + P], mk, m == 0 and s == 0,
                           m == NT - 1 and s == 1)
                for q in range(BT):
                    last = pe.matmul(bank[2][:, BT * b + q:BT * b + q + 1], mk[:, q * P:q * P + P],
                                     one16[:, :], start=(i == 0 and q == 0), stop=(m == NT - 1),
                                     skip_group_check=True)
                last.then_inc(mask_used, 1)

            def dense(b, half):
                pe.wait_ge(agg_act, b + 1)
                pe.wait_ge(agg_dve, b + 1)
                if b > 0:
                    pe.wait_ge(s_act, b)
                    pe.wait_ge(s_dve, b)
                for q in (2 * half, 2 * half + 1):
                    if q >= 2:
                        pe.wait_ge(x1_ready, BT * b + q - 1)
                    n0 = b * BN + q * P
                    o = bank[6 + q % 2]
                    for f in range(FT):
                        mm(o[:, 0:D], ST[:, f, n0:n0 + P], W12[:, f, :], f == 0, f == 1)
                    for f in range(FT):
                        last = mm(o[:, D:2 * D], H[:, f, q * P:q * P + P], W12[:, 2 + f, :], f == 0, f == 1)
                    last.then_inc(dense_ready, 1)

            def turn_h2(b):
                pe.wait_ge(h2_ready, b + 1)
                pair = H2_BANKS[b]
                for f in range(FT):
                    for q in range(BT):
                        last = pe.transpose(bank[pair + f][:, q * P:q * P + P], h2[:, q, f * P:f * P + P], ident)
                last.then_inc(h2T_ready, 1)

            for i in range(LEAD):
                turn_adj(i)
            for i in range(NT * NB):
                mean_sum(i)
                if i % NT == H2_AT and i > NT:
                    turn_h2(i // NT - 1)
                if i + LEAD < NT * NB:
                    turn_adj(i + LEAD)
                if i % NT == NT - 1:
                    dense(i // NT, 0)
                if i % NT == 1 and i > NT:
                    dense(i // NT - 1, 1)

            def spread(b, m0, m1):
                for m in range(m0, m1):
                    for s in range(2):
                        for f in range(FT):
                            l = SN[:, m, s, f * P:f * P + P]
                            first, end = m == 0 and s == 0, m == NT - 1 and s == 1
                            mm(bank[f][:, :], l, AT[:, b, m, :], first, end)
                            last = mm(bank[2 + f][:, :], l, A[:, m, b * BN:b * BN + BN], first, end)
                return last

            def bias_rows(t, r, nodes):
                mm(gate_bank[t % 4][:, :], CR[32 * r:32 * r + RR, t * P:t * P + P],
                   DR[32 * r:32 * r + RR, nodes], True, False)

            def gates(s, b, turns):
                g = NB * s + b
                nodes = slice(b * BN, b * BN + BN)
                if b > 0:
                    pe.wait_ge(gate_act, 6 * g)
                for t in range(4):
                    bias_rows(t, t, nodes)
                for t in range(4):
                    o, c = gate_bank[t][:, :], t * P
                    for f in range(FT):
                        mm(o, WG[:, 4 + f, c:c + P], ST[:, f, nodes], False, False)
                pe.wait_ge(pq_act, 2 * (g + 1))
                pe.wait_ge(pq_dve, 2 * (g + 1))
                for t in range(6):
                    o, c = gate_bank[t % 4][:, :], t * P
                    if t == 4:
                        pe.wait_ge(gate_act, 6 * g + 2)
                        for h in range(2):
                            bias_rows(4 + h, h, nodes)
                    for k in range(4):
                        last = mm(o, WG[:, k, c:c + P], PQ[:, k, :], False, t < 4 and k == 3)
                    if t >= 4:
                        if t == 4:
                            pe.wait_ge(rs_ready, 2 * (g + 1))
                        for f in range(FT):
                            last = mm(o, WG[:, 4 + f, c:c + P], RS[:, f, :], False, f == 1)
                    last.then_inc(gate_ready, 1)
                    if turns and 1 <= t <= 3:
                        if t == 3:
                            pe.wait_ge(turn_hi, 8 * s + 2)
                            pe.wait_ge(turn_lo, 8 * s + 2)
                        turn_state(t - 1, (bank[0:2], bank[2:4])[(t - 1) % 2])

            def turn_state(b, banks):
                for q in range(BT):
                    for f in range(FT):
                        n0 = b * BN + q * P
                        last = pe.transpose(banks[q // 2][:, (q % 2) * D + f * P:(q % 2) * D + f * P + P],
                                            ST[:, f, n0:n0 + P], ident)
                    if q % 2 == 1:
                        last.then_inc(turn_ready, 1)

            def step(s, final):
                for b in range(NB):
                    if b > 0:
                        spread(b, 0, NT).then_inc(agg_done, 1)
                    gates(s, b, b == NB - 1 and not final)
                if final:
                    return
                pe.wait_ge(turn_hi, 8 * s + 6)
                pe.wait_ge(turn_lo, 8 * s + 6)
                spread(0, 0, 8)
                pe.wait_ge(state_ready, 2 * NB * s + 2 * NB)
                turn_state(NB - 1, bank[6:8])
                spread(0, 8, NT - BT)
                pe.wait_ge(turn_hi, 8 * s + 8)
                pe.wait_ge(turn_lo, 8 * s + 8)
                spread(0, NT - BT, NT).then_inc(agg_done, 1)

            pe.wait_ge(agg_act, NB)
            pe.wait_ge(agg_dve, NB)
            pe.wait_ge(rdeg_ready, NB)
            pe.wait_ge(sn_hi, NB - 1)
            pe.wait_ge(sn_lo, NB - 1)
            pe.wait_ge(at_act, NT * NB // 2)
            pe.wait_ge(at_dve, NT * NB // 2)
            spread(0, 0, 2)
            dense(NB - 1, 1)
            spread(0, 2, 6)
            pe.wait_ge(s_act, NB - 1)
            pe.wait_ge(s_dve, NB - 1)
            pe.wait_ge(x1_ready, NT)
            pe.wait_ge(selL_ready, 1)
            for t in range(NT):
                last = mm(gate_bank[t // BT][0:RR, (t % BT) * P:(t % BT) * P + P], selL[:, t, :], ident, True, True)
                if t % BT == BT - 1:
                    last.then_inc(drow_ready, 1)
            spread(0, 6, 11)
            pe.wait_ge(drow_out, 2)
            turn_h2(NB - 1)
            spread(0, 11, NT - BT)
            pe.wait_ge(sn_hi, NB)
            pe.wait_ge(sn_lo, NB)
            spread(0, NT - BT, NT).then_inc(agg_done, 1)
            pe.wait_ge(s_act, NB)
            pe.wait_ge(s_dve, NB)
            pe.wait_ge(ld_rows, 16 * 6)
            pe.wait_ge(drow_out, NB)
            pe.wait_ge(ld_wg, 32)
            with pe.Fori(0, STEPS - 1) as s:
                step(s, False)
            step(STEPS - 1, True)

            pe.wait_ge(ld_o, 48)

            def out1(b):
                if b == NB - 1:
                    pe.wait_ge(state_ready, 2 * NB * STEPS)
                if b >= 2:
                    pe.wait_ge(o1_act, 2 * (b - 1))
                for o in range(2):
                    for f in range(FT):
                        last = mm(bank[2 * (b % 2) + o][:, :], wo[:, f, o * P:o * P + P],
                                  ST[:, f, b * BN:b * BN + BN], f == 0, f == 1)
                    last.then_inc(o1_ready, 1)

            def out2(b):
                pe.wait_ge(o1_act, 2 * (b + 1))
                if b == 0:
                    pe.wait_ge(gate_act, 6 * NB * STEPS)
                if b >= 2:
                    pe.wait_ge(o2_dve, 2 * (b - 1))
                for q in range(BT):
                    for o in range(2):
                        last = mm(gate_bank[2 * (b % 2) + q // 2][:, (q % 2) * D:(q % 2) * D + D],
                                  TT[:, b % 2, o, q * P:q * P + P], wo[:, o, D:2 * D], o == 0, o == 1)
                    if q % 2 == 1:
                        last.then_inc(o2_ready, 1)

            out1(0)
            for b in range(NB):
                if b + 1 < NB:
                    out1(b + 1)
                out2(b)

        @block.scalar
        def _(act):
            def copy(o, i, scale=1.0, **kw):
                return nc.scalar.activation(o, i, ACT.Copy, scale=scale, **kw)

            act.dma_start(cst[:, :], consts).then_inc(ld_c, 16)
            act.dma_start(col[:, :], cols).then_inc(ld_c, 16)
            act.dma_start(raw["rows"][0:1, :], rows).then_inc(ld_c, 16)

            def convert(k, r):
                b, c, h = k // 8, k // 2 % 4, k % 2
                if r == 0:
                    act.wait_ge(ld_ring[k % RING], 16 * (k // RING + 1))
                if k == 16:
                    act.wait_ge(crow_ready, 1)
                    act.wait_ge(st_fused, 16)
                t = BT * b + 2 * h + r
                copy(A[:, t, c * 512:c * 512 + 512], ring[:, k % RING, r, :],
                     accum_out=degA[:, t, c:c + 1]).then_inc(conv, 1)

            def move_adj(i):
                b, m = i // NT, i % NT
                act.wait_ge(tr_ready, i + 1)
                if i == NT:
                    act.wait_ge(hT_ready, NB)
                    act.wait_ge(h_lo, 4)
                if i == 2 * NT:
                    act.wait_ge(crow_out, 1)
                if i == 3 * NT:
                    act.wait_ge(st_fused, 16)
                copy(AT[:, b, m, :], bank[3 + (i + 1) % 3][:, 0:256].bitcast(FP16),
                     accum_out=degT[:, m, b:b + 1]).then_inc(at_act, 1)

            for e in range(4):
                for part, (lo, hi) in enumerate(((0, 512), (512, GATES))):
                    act.wait_ge(fused_ready, 2 * e + part + 1)
                    copy(fusedS[:, e, lo:hi], bank[4 + 2 * (e % 2) + part][:, 0:hi - lo]).then_inc(fused_out, 1)
            act.wait_ge(var_ready, 1)
            nc.scalar.activation(nrm[:, 1, :], nrm[:, 0, :], ACT.Sqrt).then_inc(sqrt_ready, 1)
            for k in range(2):
                for r in range(2):
                    convert(k, r)
            for q in range(4):
                act.wait_ge(h_ready, q + 1)
                copy(hi_lo[:, BT * q:BT * q + BT, 0, :], h32[:, BT * q:BT * q + BT, :], SCALE).then_inc(h_hi, 1)
            act.wait_ge(crow_ready, 1)
            for w in range(2):
                copy(W12[:, 2 * w:2 * w + 2, :].rearrange("p k n -> p (k n)"), bank[w][:, :])
            copy(crow[:, 0:512], bank[3][0:RR, :])
            copy(crow[:, 512:GATES], bank[2][0:RR, D:2 * D])
            copy(bias0, bank[2][:, 0:D]).then_inc(w12_out, 1)
            for q in range(4):
                act.wait_ge(hT_ready, q + 1)
                copy(ST[:, 0, q * BN:q * BN + BN], bank[4 + 2 * (q % 2)][:, :]).then_inc(hT_act, 1)

            def block_end(b):
                def sums():
                    act.wait_ge(mask_used, NT * (b + 1))
                    if b > 0:
                        act.wait_ge(h2T_ready, b)
                        act.wait_ge(sn_lo, b)
                    copy(H[:, 0, :], bank[0][:, :], 1.0 / SCALE).then_inc(agg_act, 1)

                def root():
                    act.wait_ge(var_ready, b + 2)
                    nc.scalar.activation(nrm[:, 1, 0:BT], nrm[:, 0, 0:BT], ACT.Sqrt).then_inc(sqrt_ready, 1)

                def state():
                    act.wait_ge(h2_ready, b + 1)
                    act.wait_ge(st_x1, 16 * (b + 1))
                    copy(SN[:, BT * b:BT * b + BT, 0, :], h2, SCALE).then_inc(sn_hi, 1)

                def turned():
                    act.wait_ge(h2T_ready, b + 1)
                    copy(ST[:, 0, b * BN:b * BN + BN], bank[H2_BANKS[b]][:, :]).then_inc(s_act, 1)
                return sums, root, state, turned

            for i in range(NT * NB):
                k = 2 * (i // 4 + 1) + i % 4 // 2
                if k < 8 * NB:
                    convert(k, i % 2)
                if i % NT == 0 and i:
                    block_end(i // NT - 1)[0]()
                if i % 2 == 0:
                    move_adj(i)
                if i >= NT and i % NT in STAGE_AT:
                    block_end(i // NT - 1)[1 + STAGE_AT.index(i % NT)]()
            sums, root, state, turned = block_end(NB - 1)
            for stage in (sums, root, state, turned):
                stage()

            def out_pq(g):
                act.wait_ge(agg_done, g + 1)
                for f in range(FT):
                    copy(PQ[:, f, :], bank[f][:, :], 1.0 / SCALE).then_inc(pq_act, 1)

            def turn(s, e, banks):
                for j in range(2):
                    act.wait_ge(turn_ready, 8 * s + e + j + 1)
                    t = 2 * (e + j)
                    copy(SN[:, t:t + 2, 0, :], banks[j][:, :].rearrange("p (t d) -> p t d", t=2),
                         SCALE).then_inc(turn_hi, 1)

            def step(s, final):
                for b in range(NB):
                    g = NB * s + b
                    out_pq(g)
                    for t in range(6):
                        act.wait_ge(gate_ready, 6 * g + t + 1)
                        if t == 2 and b > 0:
                            act.wait_ge(state_ready, 2 * g)
                        dst = (RS, Z, H)[t // 2][:, t % 2, :]
                        nc.scalar.activation(dst, gate_bank[t % 4][:, :],
                                             ACT.Tanh if t >= 4 else ACT.Sigmoid).then_inc(gate_act, 1)
                        if b == NB - 1 and not final and 1 <= t <= 3:
                            turn(s, 2 * (t - 1), (bank[0:2], bank[2:4])[(t - 1) % 2])
                if not final:
                    turn(s, 2 * (NB - 1), bank[6:8])

            with act.Fori(0, STEPS - 1) as s:
                step(s, False)
            step(STEPS - 1, True)
            for b in range(NB):
                for o in range(2):
                    act.wait_ge(o1_ready, 2 * b + o + 1)
                    if b >= 2:
                        act.wait_ge(o2_ready, 2 * (b - 1))
                    nc.scalar.activation(TT[:, b % 2, o, :], bank[2 * (b % 2) + o][:, :], ACT.Tanh,
                                         bias=col[:, 8 + o:9 + o]).then_inc(o1_act, 1)

        @block.vector
        def _(dve):
            v = nc.vector
            chain = [0]

            def link(ins):
                chain[0] += 1
                ins.then_inc(dve_chain, 1)
                dve.wait_ge(dve_chain, chain[0])

            def stats(tiles, base):
                for t in tiles:
                    if base == 0 and len(tiles) == NT and t % 8 == 0:
                        dve.wait_ge(ld_x[t // 8], 16)
                    ins = v.bn_stats(stat[:, t - base, :], xs[:, t, :])
                link(ins)
                for t in tiles:
                    ins = v.bn_aggr(mv[:, t - base, :], stat[:, t - base, :])
                link(ins)
                n = len(tiles)
                v.tensor_scalar(nrm[:, 0, 0:n], mv[:, 0:n, 1], EPS, None, ALU.add).then_inc(var_ready, 1)

            stats(range(NT), 0)
            dve.wait_ge(ld_c, 48)
            link(v.tensor_copy(id16[:, :], cst[:, C_ID:C_ID + P]))
            v.tensor_copy(one16[:, :], cst[:, C_ONE:C_ONE + 1]).then_inc(id16_ready, 1)
            for j in range(4):
                v.tensor_scalar(L0[:, j, :], one_col, col[:, 4 + j:5 + j], None, ALU.mult)
                v.tensor_scalar(Lr[:, j, :], cst[:, C_SEL + RR * (j // 2):C_SEL + RR * (j // 2 + 1)],
                                col[:, j:j + 1], None, ALU.mult)
            v.tensor_copy(raw["Lb"][0:1, :], cst[0:1, C_SEL + 2 * RR:C_SEL + 3 * RR]).then_inc(left_ready, 1)

            def newton(n, count):
                dve.wait_ge(sqrt_ready, count)
                ve, rt, sc, rs = (nrm[:, j, 0:n] for j in range(4))
                link(v.reciprocal(sc, rt))
                link(v.tensor_tensor(sc, sc, ve, ALU.mult))
                link(v.tensor_tensor(sc, sc, rt, ALU.add))
                link(v.tensor_scalar(sc, sc, 0.5, None, ALU.mult))
                link(v.reciprocal(rs, sc))

            newton(NT, 1)
            for q in range(4):
                for t in range(BT * q, BT * q + BT):
                    ins = v.tensor_scalar(h32[:, t, :], xs[:, t, :], mv[:, t, 0:1], nrm[:, 3, t:t + 1],
                                          ALU.subtract, ALU.mult)
                link(ins)
                hq = h32[:, BT * q:BT * q + BT, :].rearrange("p t d -> p (t d)")
                v.tensor_scalar(hq, hq, 0.0, None, ALU.max).then_inc(h_ready, 1)
            for q in range(4):
                dve.wait_ge(h_hi, q + 1)
                v.scalar_tensor_tensor(out=hi_lo[:, BT * q:BT * q + BT, 1, :], in0=h32[:, BT * q:BT * q + BT, :],
                                       scalar=SCALE, in1=hi_lo[:, BT * q:BT * q + BT, 0, :],
                                       op0=ALU.mult, op1=ALU.subtract).then_inc(h_lo, 1)
                dve.wait_ge(hT_ready, q + 1)
                v.tensor_copy(ST[:, 1, q * BN:q * BN + BN], bank[5 + 2 * (q % 2)][:, :]).then_inc(hT_dve, 1)

            def split_rows(dst, src, tmp, keep):
                n = dst.shape[1]
                rest = tmp[0:RR, 0:n]
                piece = tmp[0:RR, n:n + n // 2].bitcast(BF16)
                k1, k2 = (cst[0:RR, keep + j:keep + j + 1] for j in range(2))
                link(v.tensor_copy(piece, src))
                link(v.scalar_tensor_tensor(out=rest, in0=piece, scalar=k1, in1=src, op0=ALU.mult,
                                            op1=ALU.subtract))
                link(v.tensor_copy(piece, rest))
                return v.scalar_tensor_tensor(out=dst, in0=piece, scalar=k2, in1=rest, op0=ALU.mult,
                                              op1=ALU.subtract)

            def move_adj(i):
                b, m = i // NT, i % NT
                dve.wait_ge(tr_ready, i + 1)
                if i == 3 * NT + 1:
                    dve.wait_ge(st_fused, 16)
                v.tensor_scalar(AT[:, b, m, :], bank[3 + (i + 1) % 3][:, 0:256].bitcast(FP16), 1.0, None, ALU.mult,
                                ALU.add, accum_out=degT[:, m, b:b + 1]).then_inc(at_dve, 1)

            def make_mask(i):
                b, m = i // NT, i % NT
                if i % 2 == 0:
                    dve.wait_ge(at_act, i // 2 + 1)
                else:
                    dve.wait_ge(at_dve, i // 2 + 1)
                if i >= 4:
                    dve.wait_ge(mask_used, i - 3)
                v.tensor_scalar(mask[:, i % 4, :], AT[:, b, m, :], 0.0, None, ALU.is_gt).then_inc(mask_ready, 1)

            def sums(b):
                dve.wait_ge(mask_used, NT * (b + 1))
                if b > 0:
                    dve.wait_ge(h2T_ready, b)
                    dve.wait_ge(sn_hi, b)
                v.tensor_scalar(H[:, 1, :], bank[1][:, :], 1.0 / SCALE, None, ALU.mult).then_inc(agg_dve, 1)
                tiles = slice(BT * b, BT * b + BT)
                v.tensor_scalar(rdeg[:, tiles], bank[2][:, tiles], 1.0, None, ALU.max).then_inc(rdeg_ready, 1)
                dve.wait_ge(rdeg_ready, b + 1)
                link(v.reciprocal(rdeg[:, tiles], rdeg[:, tiles]))

            def residual(b, half):
                for q in (2 * half, 2 * half + 1):
                    t = BT * b + q
                    o = bank[6 + q % 2]
                    u = u_tmp[:, :]
                    dve.wait_ge(dense_ready, t + 1)
                    link(v.scalar_tensor_tensor(out=u, in0=o[:, D:2 * D], scalar=rdeg[:, t:t + 1], in1=bias0,
                                                op0=ALU.mult, op1=ALU.add))
                    link(v.tensor_tensor(u, u, o[:, 0:D], ALU.add))
                    v.scalar_tensor_tensor(out=xs[:, t, :], in0=u, scalar=0.0, in1=xs[:, t, :],
                                           op0=ALU.max, op1=ALU.add).then_inc(x1_ready, 1)
                    dve.wait_ge(x1_ready, t + 1)

            def normed(b):
                newton(BT, b + 2)
                dve.wait_ge(dense_ready, BT * (b + 1))
                for q in range(BT):
                    ins = v.tensor_scalar(h2[:, q, :], xs[:, BT * b + q, :], mv[:, q, 0:1], nrm[:, 3, q:q + 1],
                                          ALU.subtract, ALU.mult)
                link(ins)
                v.tensor_scalar(Hf, Hf, 0.0, None, ALU.max).then_inc(h2_ready, 1)

            def state(b):
                dve.wait_ge(sn_hi, b + 1)
                tiles = slice(BT * b, BT * b + BT)
                v.scalar_tensor_tensor(out=SN[:, tiles, 1, :], in0=h2, scalar=SCALE, in1=SN[:, tiles, 0, :],
                                       op0=ALU.mult, op1=ALU.subtract).then_inc(sn_lo, 1)

            def turned(b):
                dve.wait_ge(h2T_ready, b + 1)
                v.tensor_copy(ST[:, 1, b * BN:b * BN + BN], bank[H2_BANKS[b] + 1][:, :]).then_inc(s_dve, 1)

            for i in range(NT * NB + 1):
                if i:
                    make_mask(i - 1)
                if i % NT == 0 and i:
                    sums(i // NT - 1)
                if i % 2 == 1:
                    move_adj(i)
                if i == 12:
                    dve.wait_ge(w12_out, 1)
                    split_rows(CR[0:RR, :], crow, ctmp, C_KC).then_inc(crow_out, 1)
                if i > NT and i % NT in (2, 4):
                    residual(i // NT - 1, i % NT // 4)
                if i > NT and i % NT == 5:
                    b = i // NT - 1
                    stats(range(BT * b, BT * b + BT), BT * b)
                if i > NT and i % NT == STAGE_AT[0] + 1:
                    normed(i // NT - 1)
                if i > NT and i % NT == STAGE_AT[1] + 1:
                    state(i // NT - 1)
                if i > NT and i % NT == STAGE_AT[2] + 1:
                    turned(i // NT - 1)
            for half in range(2):
                residual(NB - 1, half)
            dve.wait_ge(conv, 4 * NT)
            dve.wait_ge(at_act, NT * NB // 2)
            v.tensor_reduce(degs[:, 0, :], degA[:, :, :], mybir.AxisListType.X, ALU.add)
            v.tensor_reduce(degs[:, 1, :], degT[:, :, :], mybir.AxisListType.X, ALU.add)
            stats(range(BT * (NB - 1), NT), BT * (NB - 1))
            wide = [P, NT, RR]
            sel = [cst[:, C_SEL + RR * j:C_SEL + RR * (j + 1)].unsqueeze(1).broadcast_to(wide) for j in range(3)]
            deg = [degs[:, j, :].unsqueeze(2).broadcast_to(wide) for j in range(2)]
            selT = f32w[:, 3072:3072 + NT * RR].rearrange("p (t r) -> p t r", t=NT)
            v.tensor_tensor(selL[:, :, :], deg[0], sel[0], ALU.mult)
            link(v.tensor_tensor(selT, deg[1], sel[1], ALU.mult))
            link(v.tensor_tensor(selL[:, :, :], selL[:, :, :], selT, ALU.add))
            v.tensor_tensor(selL[:, :, :], selL[:, :, :], sel[2], ALU.add).then_inc(selL_ready, 1)
            normed(NB - 1)
            for b in range(NB):
                dve.wait_ge(drow_ready, b + 1)
                split_rows(DR[0:RR, b * BN:b * BN + BN], gate_bank[b][0:RR, :], f32w[:, 3072:4096],
                           C_KD).then_inc(drow_out, 1)
                dve.wait_ge(drow_out, b + 1)
            state(NB - 1)
            turned(NB - 1)

            def out_pq(g):
                dve.wait_ge(agg_done, g + 1)
                for f in range(FT):
                    v.tensor_scalar(PQ[:, 2 + f, :], bank[2 + f][:, :], 1.0 / SCALE, None,
                                    ALU.mult).then_inc(pq_dve, 1)

            def turn(s, e, banks):
                for j in range(2):
                    dve.wait_ge(turn_hi, 8 * s + e + j + 1)
                    t = 2 * (e + j)
                    v.scalar_tensor_tensor(out=SN[:, t:t + 2, 1, :],
                                           in0=banks[j][:, :].rearrange("p (t d) -> p t d", t=2),
                                           scalar=SCALE, in1=SN[:, t:t + 2, 0, :],
                                           op0=ALU.mult, op1=ALU.subtract).then_inc(turn_lo, 1)

            base = chain[0]
            PER_BLOCK = 4

            def step(s, final):
                for b in range(NB):
                    g = NB * s + b
                    nodes = slice(b * BN, b * BN + BN)
                    out_pq(g)
                    for f in range(FT):
                        dve.wait_ge(gate_act, 6 * g + f + 1)
                        v.tensor_tensor(RS[:, f, :], RS[:, f, :], ST[:, f, nodes], ALU.mult).then_inc(rs_ready, 1)
                    if b == NB - 1 and not final:
                        for e in range(3):
                            turn(s, 2 * e, (bank[0:2], bank[2:4])[e % 2])
                    for f in range(FT):
                        c = base + PER_BLOCK * g + 2 * f
                        dve.wait_ge(gate_act, 6 * g + 5 + f)
                        v.tensor_tensor(H[:, f, :], H[:, f, :], ST[:, f, nodes],
                                        ALU.subtract).then_inc(dve_chain, 1)
                        dve.wait_ge(dve_chain, c + 1)
                        v.tensor_tensor(H[:, f, :], H[:, f, :], Z[:, f, :], ALU.mult).then_inc(dve_chain, 1)
                        dve.wait_ge(dve_chain, c + 2)
                        v.tensor_tensor(ST[:, f, nodes], ST[:, f, nodes], H[:, f, :],
                                        ALU.add).then_inc(state_ready, 1)
                if not final:
                    turn(s, 2 * (NB - 1), bank[6:8])

            with dve.Fori(0, STEPS - 1) as s:
                step(s, False)
            step(STEPS - 1, True)
            dve.wait_ge(ld_o, 48)
            for t in range(NT):
                ins = v.tensor_tensor(x1o[:, t, :], x1o[:, t, :], ob, ALU.add)
            ins.then_inc(dve_chain, 1)
            dve.wait_ge(dve_chain, base + PER_BLOCK * NB * STEPS + 1)
            for e in range(2 * NB):
                dve.wait_ge(o2_ready, e + 1)
                tiles = slice(2 * e, 2 * e + 2)
                v.tensor_tensor(res[:, tiles, :].rearrange("p t d -> p (t d)"),
                                gate_bank[e % 4][:, :],
                                x1o[:, tiles, :].rearrange("p t d -> p (t d)"), ALU.add).then_inc(o2_dve, 1)


def kernel(**inputs):
    import numpy as np
    import concourse.bacc as bacc
    from concourse.bass_utils import run_bass_kernel_spmd

    a = {k: np.asarray(v) for k, v in inputs.items()}
    f = np.float32
    consts = np.zeros((P, C_END), f)
    consts[:, C_ID:C_ID + P] = np.eye(P, dtype=f)
    consts[:, C_ONE:C_ONE + P] = 1.0
    for j, (lo, hi) in enumerate(((0, 9), (9, 18), (18, RR))):
        consts[:, C_SEL + RR * j + lo:C_SEL + RR * j + hi] = 1.0
    for k in range(RR):
        c, d = k % 3, (k % 9 // 3 if k < 18 else 0)
        consts[k, C_KC:C_KC + 2] = c >= 1, c >= 2
        consts[k, C_KD:C_KD + 2] = d >= 1, d >= 2
    two = lambda v: v.reshape(2, P).T
    arrays = {
        "x": a["x"], "adj": a["adj"],
        "w_in": a["L1_gnn_in_W"], "w_out": a["L1_gnn_out_W"],
        "wg_t": np.concatenate([a["L1_gnn_r_W"].T, a["L1_gnn_z_W"].T, a["L1_gnn_h_W"].T], 1),
        "w0_t": np.concatenate([a["L0_gnn_W_self"].T, a["L0_gnn_W_nb"].T], 1),
        "w_comb": a["L0_gnn_W_comb"],
        "w_o": np.concatenate([a["L1_gnn_o1_W"].T, a["L1_gnn_o2_W"].T], 1),
        "cols": np.concatenate([two(a["L1_gnn_in_b"]), two(a["L1_gnn_out_b"]), two(a["L0_gnn_b_self"]),
                                two(a["L0_gnn_b_nb"]), two(a["L1_gnn_o1_b"])], 1),
        "rows": np.concatenate([a["L1_gnn_r_b"], a["L1_gnn_z_b"], a["L1_gnn_h_b"], a["L0_gnn_b_comb"]])[None],
        "o2_b": a["L1_gnn_o2_b"],
        "consts": consts,
    }
    arrays = {k: np.ascontiguousarray(v) for k, v in arrays.items()}
    nc = bacc.Bacc("TRN2", target_bir_lowering=False, num_devices=1)
    args = [nc.dram_tensor(f"in_{k}", v.shape, mybir.dt.from_np(v.dtype), kind="ExternalInput").ap()
            for k, v in arrays.items()]
    out = nc.dram_tensor("out", (N, D), FP32, kind="ExternalOutput").ap()
    graph_net(nc, *args, out)
    r = run_bass_kernel_spmd(nc, [{f"in_{k}": v for k, v in arrays.items()}], core_ids=[0])
    return r.results[0]["out"]
```

```python
import concourse.bass as bass
from concourse import mybir
from contextlib import ExitStack

FP32 = mybir.dt.float32
FP16 = mybir.dt.float16
INT32 = mybir.dt.int32
ALU = mybir.AluOpType
ACT = mybir.ActivationFunctionType

P = 128
N = 2048
D = 256
NT = N // P
FT = D // P
NB = 4
BN = N // NB
BT = BN // P
GATES = 3 * D
KG = 6
STEPS = 5
SCALE = 2.0 ** 11
EPS = 1e-5
RING = 3
LEAD = 3
C_ID, C_ONE, C_END = 0, P, 2 * P
STAGE_AT = [8, 13, 14]
H2_AT = 12
H2_BANKS = [6, 6, 6, 4]


def graph_net(nc, x, adj, w_in, w_out, wg_t, w0_t, w_comb, w_o, cols, b_comb, o2_b, consts, out):
    ctx = ExitStack()
    with ctx:
        def sb(name, shape, dt):
            return ctx.enter_context(nc.sbuf_tensor(name, shape, dt))

        def sem(name):
            return ctx.enter_context(nc.semaphore(name))

        fused_d = nc.dram_tensor("fused_d", [P, 4, GATES], FP32, kind="Internal").ap()
        x1_d = nc.dram_tensor("x1_d", [P, NT, D], FP32, kind="Internal").ap()

        A = sb("A", [P, NT, N], FP16)
        AT = sb("AT", [P, NB, NT, BN], FP16)
        ST = sb("ST", [P, FT, N], FP32)
        SN = sb("SN", [P, NT, 2, D], FP16)
        work = sb("work", [P, 16384], mybir.dt.uint8)
        H = sb("H", [P, FT, BN], FP32)
        WG = sb("WG", [P, KG, GATES], FP32)
        masks_degA = sb("masks_degA", [P, N], FP16)
        cst = sb("cst", [P, C_END], FP32)
        id16 = sb("id16", [P, P], FP16)
        col = sb("col", [P, 16], FP32)
        gcol = sb("gcol", [P, 2, 6], FP32)
        degA = sb("degA", [P, NT, 4], FP32)
        degT = sb("degT", [P, NT, NB], FP32)
        degs = sb("degs", [P, 2, NT], FP32)
        rdeg = sb("rdeg", [P, NT], FP32)
        stat = sb("stat", [P, NT, 6], FP32)
        mv = sb("mv", [P, NT, 2], FP32)
        nrm = sb("nrm", [P, 4, NT], FP32)
        one16 = sb("one16", [P, P], FP16)

        hi_lo = work[:, :].bitcast(FP16).rearrange("p (t s d) -> p t s d", t=NT, s=2)
        f32w = work[:, :].bitcast(FP32)
        PQ = f32w[:, 0:2048].rearrange("p (k n) -> p k n", k=4)
        RS = f32w[:, 2048:3072].rearrange("p (k n) -> p k n", k=2)
        Z = f32w[:, 3072:4096].rearrange("p (k n) -> p k n", k=2)
        cand = PQ[:, 0:2, :]
        diag = work[:, 8192:16384].bitcast(FP16).rearrange("p (w t n) -> p w t n", w=2, t=NT)
        xs = SN[:, :, :, :].rearrange("p t s d -> p t (s d)").bitcast(FP32)
        wflat = WG[:, :, :].rearrange("p k n -> p (k n)")
        ring = wflat[:, 0:RING * 1024].bitcast(INT32).rearrange("p (s r w) -> p s r w", s=RING, r=2)
        W12 = wflat[:, 3072:4096].rearrange("p (k n) -> p k n", k=4)
        bias0 = wflat[:, 4096:4096 + D]
        u_tmp = wflat[:, 4096 + D:4096 + 2 * D]
        mask = masks_degA[:, :].rearrange("p (r n) -> p r n", r=4)
        degA_all = masks_degA[:, :]
        degT_all = H[:, :, :].rearrange("p k n -> p (k n)").bitcast(FP16)
        h2 = H[:, :, :].rearrange("p k n -> p (k n)").rearrange("p (q d) -> p q d", q=BT)
        Hf = H[:, :, :].rearrange("p k n -> p (k n)")
        one_col = cst[:, C_ONE:C_ONE + P]

        lateA = A[:, 8:16, :].rearrange("p t n -> p (t n)").bitcast(FP32)
        at = 0
        raw = {}
        for name, size in (("wg", 4 * GATES), ("io", 4 * D), ("w0", 4 * D), ("wc", 4 * D),
                           ("b_comb", D), ("L0", 4 * P)):
            raw[name] = lateA[:, at:at + size]
            at += size
        assert at <= 8192
        wgR = raw["wg"].rearrange("p (k n) -> p k n", k=4)
        ioR = raw["io"].rearrange("p (w j f) -> p w j f", w=2, j=2)
        w0R = raw["w0"].rearrange("p (j n) -> p j n", j=2)
        wcR = raw["wc"].rearrange("p (j n) -> p j n", j=4)
        L0 = raw["L0"].rearrange("p (k r) -> p k r", k=4)
        h32 = AT[:, 1, :, :].rearrange("p t n -> p (t n)").bitcast(FP32).rearrange("p (t d) -> p t d", t=NT)
        fusedS = AT[:, 3, :, :].rearrange("p t n -> p (t n)").bitcast(FP32)[:, 0:4 * GATES].rearrange(
            "p (k n) -> p k n", k=4)
        freeA = A[:, :, :].rearrange("p t n -> p (t n)").bitcast(FP32)
        x1o = freeA[:, 0:4096].rearrange("p (t d) -> p t d", t=NT)
        res = freeA[:, 4096:8192].rearrange("p (t d) -> p t d", t=NT)
        TT = freeA[:, 8192:10240].rearrange("p (v k n) -> p v k n", v=2, k=2)
        wo = freeA[:, 10240:11264].rearrange("p (k n) -> p k n", k=2)
        ob = freeA[:, 11264:11264 + D]

        bank = [ctx.enter_context(nc.psum_tensor(f"bank{i}", [P, 512], FP32)) for i in range(8)]
        gate_bank = bank[4:8]

        ld_c, ld_w0, ld_o = sem("ld_c"), sem("ld_w0"), sem("ld_o")
        ld_w = [sem(f"ld_w_{w}") for w in ("in", "out")]
        ld_x = [sem(f"ld_x{i}") for i in range(2)]
        ld_ring = [sem(f"ld_ring{i}") for i in range(RING)]
        ld_wg = sem("ld_wg")
        st_fused, st_x1, st_out = sem("st_fused"), sem("st_x1"), sem("st_out")
        id16_ready = sem("id16_ready")
        left_ready = sem("left_ready")
        fused_ready = sem("fused_ready")
        fused_out = sem("fused_out")
        w12_out = sem("w12_out")
        setup_done = sem("setup_done")
        var_ready, sqrt_ready = sem("var_ready"), sem("sqrt_ready")
        h_ready = sem("h_ready")
        h_hi, h_lo = sem("h_hi"), sem("h_lo")
        hT_ready, hT_act, hT_dve = sem("hT_ready"), sem("hT_act"), sem("hT_dve")
        conv = sem("conv")
        tr_ready = sem("tr_ready")
        at_act, at_dve = sem("at_act"), sem("at_dve")
        mask_ready, mask_used = sem("mask_ready"), sem("mask_used")
        agg_act, agg_dve = sem("agg_act"), sem("agg_dve")
        rdeg_ready = sem("rdeg_ready")
        dense_ready, x1_ready = sem("dense_ready"), sem("x1_ready")
        h2_ready, h2T_ready = sem("h2_ready"), sem("h2T_ready")
        s_act, s_dve = sem("s_act"), sem("s_dve")
        sn_hi, sn_lo = sem("sn_hi"), sem("sn_lo")
        diag_ready = sem("diag_ready")
        deg_ready, deg_out = sem("deg_ready"), sem("deg_out")
        agg_done = sem("agg_done")
        pq_act, pq_dve = sem("pq_act"), sem("pq_dve")
        gate_ready, gate_dve, gate_act = sem("gate_ready"), sem("gate_dve"), sem("gate_act")
        rs_ready, state_ready = sem("rs_ready"), sem("state_ready")
        turn_ready, turn_hi, turn_lo = sem("turn_ready"), sem("turn_hi"), sem("turn_lo")
        o1_ready, o1_act, o2_ready, o2_dve = sem("o1_ready"), sem("o1_act"), sem("o2_ready"), sem("o2_dve")
        dve_chain = sem("dve_chain")

        block = ctx.enter_context(nc.Block())

        @block.sync
        def _(sp):
            x_v = x.rearrange("(t p) d -> p t d", p=P)
            for w, w_half in enumerate((w_in, w_out)):
                sp.dma_start(ioR[:, w], w_half.rearrange("(j p) f -> p j f", p=P)).then_inc(ld_w[w], 16)
                sp.dma_start(wgR[:, 2 * w:2 * w + 2, :],
                             wg_t[w * D:w * D + D, :].rearrange("(k p) n -> p k n", p=P)).then_inc(ld_w[w], 16)
            for h in range(2):
                sp.dma_start(xs[:, 8 * h:8 * h + 8, :], x_v[:, 8 * h:8 * h + 8, :]).then_inc(ld_x[h], 16)
            sp.dma_start(w0R, w0_t.rearrange("(j p) n -> p j n", p=P)).then_inc(ld_w0, 16)
            sp.dma_start(wcR, w_comb.rearrange("(j p) n -> p j n", p=P)).then_inc(ld_w0, 16)
            adj_v = adj.rearrange("(b h r p) (c w) -> b c h p r w", b=NB, h=2, r=2, p=P, c=4)
            for k in range(2 * 4 * NB):
                b, c, h = k // 8, k // 2 % 4, k % 2
                if k >= RING:
                    sp.wait_ge(conv, 2 * (k - RING + 1))
                sp.dma_start(ring[:, k % RING, :, :], adj_v[b, c, h]).then_inc(ld_ring[k % RING], 16)
            sp.wait_ge(conv, 4 * NT)
            sp.wait_ge(dense_ready, NT)
            sp.wait_ge(st_x1, 16 * NB)
            sp.wait_ge(st_fused, 16)
            sp.dma_start(WG[:, 0:4, :], fused_d).then_inc(ld_wg, 16)
            sp.dma_start(WG[:, 4:6, :], wg_t[2 * D:3 * D, :].rearrange("(k p) n -> p k n", p=P)).then_inc(ld_wg, 16)
            sp.wait_ge(agg_done, NB * STEPS)
            sp.dma_start(wo, w_o.rearrange("(k p) n -> p k n", p=P)).then_inc(ld_o, 16)
            sp.dma_start(x1o, x1_d).then_inc(ld_o, 16)
            sp.dma_start(ob, o2_b.partition_broadcast(P)).then_inc(ld_o, 16)
            out_v = out.rearrange("(t p) d -> p t d", p=P)
            for b in range(NB):
                sp.wait_ge(o2_dve, 2 * (b + 1))
                sp.dma_start(out_v[:, BT * b:BT * b + BT, :], res[:, BT * b:BT * b + BT, :]).then_inc(st_out, 16)
            sp.wait_ge(st_out, 16 * NB)

        @block.gpsimd
        def _(pool):
            pool.wait_ge(fused_out, 8)
            pool.dma_start(fused_d, fusedS).then_inc(st_fused, 16)
            for b in range(NB):
                pool.wait_ge(x1_ready, BT * (b + 1))
                pool.dma_start(x1_d[:, BT * b:BT * b + BT, :], xs[:, BT * b:BT * b + BT, :]).then_inc(st_x1, 16)

        @block.tensor
        def _(pe):
            ident = cst[:, C_ID:C_ID + P]

            def mm(o, l, r, start, stop):
                return pe.matmul(o, l, r, start=start, stop=stop)

            for e in range(4):
                w, f = e // 2, e % 2
                if f == 0:
                    pe.wait_ge(ld_w[w], 32)
                if e >= 2:
                    pe.wait_ge(fused_out, 2 * (e - 1))
                for part, (lo, hi) in enumerate(((0, 512), (512, GATES))):
                    for j in range(2):
                        last = mm(bank[4 + 2 * (e % 2) + part][:, 0:hi - lo], ioR[:, w, j, f * P:f * P + P],
                                  wgR[:, 2 * w + j, lo:hi], j == 0, j == 1)
                    last.then_inc(fused_ready, 1)

            def turn_h(b):
                pe.wait_ge(h_ready, b + 1)
                if b < 2:
                    pe.wait_ge(fused_out, 2 * b + 6)
                else:
                    pe.wait_ge(hT_act, b - 1)
                    pe.wait_ge(hT_dve, b - 1)
                for f in range(FT):
                    for q in range(BT):
                        last = pe.transpose(bank[4 + 2 * (b % 2) + f][:, q * P:q * P + P],
                                            h32[:, BT * b + q, f * P:f * P + P], ident)
                last.then_inc(hT_ready, 1)

            pe.wait_ge(ld_c, 48)
            pe.wait_ge(ld_w0, 32)
            for w in range(2):
                for i in range(2):
                    for j in range(2):
                        last = mm(bank[w][:, i * D:i * D + D], w0R[:, j, w * D + i * P:w * D + i * P + P],
                                  wcR[:, 2 * w + j, :], j == 0, j == 1)
            pe.wait_ge(left_ready, 1)
            for j in range(4):
                mm(bank[2][:, 0:D], L0[:, j, :], wcR[:, j, :], j == 0, False)
            mm(bank[2][:, 0:D], cst[0:1, C_ONE:C_ONE + P], raw["b_comb"][0:1, :], False, True)
            turn_h(0)
            turn_h(1)
            for w in range(2):
                for t in range(6):
                    for j in range(2):
                        last = mm(bank[3][:, 6 * w + t:6 * w + t + 1], wgR[:, 2 * w + j, t * P:t * P + P],
                                  col[:, 2 * w + j:2 * w + j + 1], j == 0, j == 1)
            last.then_inc(setup_done, 1)
            turn_h(2)
            turn_h(3)

            def turn_adj(i):
                b, m = i // NT, i % NT
                pe.wait_ge(conv, 4 * (4 * b + m // 4 + 1))
                if i == 2:
                    pe.wait_ge(w12_out, 1)
                if i == 0:
                    pe.wait_ge(id16_ready, 1)
                    pe.wait_ge(hT_act, NB)
                    pe.wait_ge(hT_dve, NB)
                if i >= 3:
                    if i % 2 == 1:
                        pe.wait_ge(at_act, (i - 3) // 2 + 1)
                    else:
                        pe.wait_ge(at_dve, (i - 3) // 2 + 1)
                o = bank[3 + (i + 1) % 3][:, 0:256].bitcast(FP16)
                for q in range(BT):
                    last = pe.transpose(o[:, q * P:q * P + P], A[:, BT * b + q, m * P:m * P + P], id16[:, :])
                last.then_inc(tr_ready, 1)

            def mean_sum(i):
                b, m = i // NT, i % NT
                pe.wait_ge(mask_ready, i + 1)
                if m == 0 and b == 0:
                    pe.wait_ge(h_hi, 4)
                    pe.wait_ge(h_lo, 4)
                    pe.wait_ge(w12_out, 1)
                if m == 0 and b > 0:
                    pe.wait_ge(agg_act, b)
                    pe.wait_ge(agg_dve, b)
                    pe.wait_ge(rdeg_ready, b)
                mk = mask[:, i % 4, :]
                for s in range(2):
                    for f in range(FT):
                        mm(bank[f][:, :], hi_lo[:, m, s, f * P:f * P + P], mk, m == 0 and s == 0,
                           m == NT - 1 and s == 1)
                for q in range(BT):
                    last = pe.matmul(bank[2][:, BT * b + q:BT * b + q + 1], mk[:, q * P:q * P + P],
                                     one16[:, 0:1], start=(i == 0 and q == 0), stop=(m == NT - 1),
                                     skip_group_check=True)
                last.then_inc(mask_used, 1)

            def dense(b, half):
                pe.wait_ge(agg_act, b + 1)
                pe.wait_ge(agg_dve, b + 1)
                if b > 0:
                    pe.wait_ge(s_act, b)
                    pe.wait_ge(s_dve, b)
                for q in (2 * half, 2 * half + 1):
                    if q >= 2:
                        pe.wait_ge(x1_ready, BT * b + q - 1)
                    n0 = b * BN + q * P
                    o = bank[6 + q % 2]
                    for f in range(FT):
                        mm(o[:, 0:D], ST[:, f, n0:n0 + P], W12[:, f, :], f == 0, f == 1)
                    for f in range(FT):
                        last = mm(o[:, D:2 * D], H[:, f, q * P:q * P + P], W12[:, 2 + f, :], f == 0, f == 1)
                    last.then_inc(dense_ready, 1)

            def turn_h2(b):
                pe.wait_ge(h2_ready, b + 1)
                pair = H2_BANKS[b]
                for f in range(FT):
                    for q in range(BT):
                        last = pe.transpose(bank[pair + f][:, q * P:q * P + P], h2[:, q, f * P:f * P + P], ident)
                last.then_inc(h2T_ready, 1)

            for i in range(LEAD):
                turn_adj(i)
            for i in range(NT * NB):
                mean_sum(i)
                if i % NT == H2_AT and i > NT:
                    turn_h2(i // NT - 1)
                if i + LEAD < NT * NB:
                    turn_adj(i + LEAD)
                if i % NT == NT - 1:
                    dense(i // NT, 0)
                if i % NT == 1 and i > NT:
                    dense(i // NT - 1, 1)

            def spread(b, m0, m1):
                def node_tile(m, first, end):
                    for s in range(2):
                        for f in range(FT):
                            l = SN[:, m, s, f * P:f * P + P]
                            start, stop = first and s == 0, end and s == 1
                            mm(bank[f][:, :], l, AT[:, b, m, :], start, stop)
                            last = mm(bank[2 + f][:, :], l, A[:, m, b * BN:b * BN + BN], start, stop)
                    return last

                node_tile(m0, m0 == 0, False)
                if m0 + 1 < min(m1, NT - 1):
                    with pe.Fori(m0 + 1, min(m1, NT - 1)) as m:
                        node_tile(m, False, False)
                if m1 == NT:
                    last = node_tile(NT - 1, False, True)
                    return last

            def spread_degrees(w):
                for t in range(NT):
                    last = mm(gate_bank[t // BT][:, (t % BT) * P:(t % BT) * P + P], one16[:, :],
                              diag[:, w, t, :], True, True)
                    if t % BT == BT - 1:
                        last.then_inc(deg_ready, 1)

            def gates(s, b, turns):
                g = NB * s + b
                nodes = slice(b * BN, b * BN + BN)
                if b > 0:
                    pe.wait_ge(gate_dve, 6 * g)
                for t in range(4):
                    for f in range(FT):
                        mm(gate_bank[t][:, :], WG[:, 4 + f, t * P:t * P + P], ST[:, f, nodes], f == 0, False)
                pe.wait_ge(pq_act, 2 * (g + 1))
                pe.wait_ge(pq_dve, 2 * (g + 1))
                for t in range(4):
                    for k in range(4):
                        last = mm(gate_bank[t][:, :], WG[:, k, t * P:t * P + P], PQ[:, k, :], False, k == 3)
                    last.then_inc(gate_ready, 1)
                    if turns and t >= 1:
                        if t == 3:
                            pe.wait_ge(turn_hi, 8 * s + 2)
                            pe.wait_ge(turn_lo, 8 * s + 2)
                        turn_state(t - 1, (bank[0:2], bank[2:4])[(t - 1) % 2])
                pe.wait_ge(gate_dve, 6 * g + 2)
                for t in (4, 5):
                    for k in range(4):
                        mm(gate_bank[t - 4][:, :], WG[:, k, t * P:t * P + P], PQ[:, k, :], k == 0, False)
                pe.wait_ge(rs_ready, 2 * (g + 1))
                for t in (4, 5):
                    for f in range(FT):
                        last = mm(gate_bank[t - 4][:, :], WG[:, 4 + f, t * P:t * P + P], RS[:, f, :], False, f == 1)
                    last.then_inc(gate_ready, 1)

            def turn_state(b, banks):
                for q in range(BT):
                    for f in range(FT):
                        n0 = b * BN + q * P
                        last = pe.transpose(banks[q // 2][:, (q % 2) * D + f * P:(q % 2) * D + f * P + P],
                                            ST[:, f, n0:n0 + P], ident)
                    if q % 2 == 1:
                        last.then_inc(turn_ready, 1)

            def step(s, final):
                for b in range(NB):
                    if b > 0:
                        spread(b, 0, NT).then_inc(agg_done, 1)
                    gates(s, b, b == NB - 1 and not final)
                if final:
                    return
                pe.wait_ge(turn_hi, 8 * s + 6)
                pe.wait_ge(turn_lo, 8 * s + 6)
                spread(0, 0, 8)
                pe.wait_ge(state_ready, 2 * NB * s + 2 * NB)
                turn_state(NB - 1, bank[6:8])
                spread(0, 8, NT - BT)
                pe.wait_ge(turn_hi, 8 * s + 8)
                pe.wait_ge(turn_lo, 8 * s + 8)
                spread(0, NT - BT, NT).then_inc(agg_done, 1)

            pe.wait_ge(agg_act, NB)
            pe.wait_ge(agg_dve, NB)
            pe.wait_ge(rdeg_ready, NB)
            pe.wait_ge(sn_hi, NB - 1)
            pe.wait_ge(sn_lo, NB - 1)
            pe.wait_ge(at_act, NT * NB // 2)
            pe.wait_ge(at_dve, NT * NB // 2)
            spread(0, 0, 2)
            dense(NB - 1, 1)
            spread(0, 2, 8)
            pe.wait_ge(s_act, NB - 1)
            pe.wait_ge(s_dve, NB - 1)
            pe.wait_ge(x1_ready, NT)
            pe.wait_ge(diag_ready, 1)
            spread_degrees(0)
            spread(0, 8, 10)
            pe.wait_ge(deg_out, 2)
            turn_h2(NB - 1)
            spread(0, 10, 11)
            pe.wait_ge(deg_out, NB)
            pe.wait_ge(s_act, NB)
            pe.wait_ge(s_dve, NB)
            spread_degrees(1)
            spread(0, 11, NT - BT)
            pe.wait_ge(sn_hi, NB)
            pe.wait_ge(sn_lo, NB)
            spread(0, NT - BT, NT).then_inc(agg_done, 1)
            pe.wait_ge(deg_out, 2 * NB)
            pe.wait_ge(ld_wg, 32)
            with pe.Fori(0, STEPS - 1) as s:
                step(s, False)
            step(STEPS - 1, True)

            pe.wait_ge(ld_o, 48)

            def out1(b):
                if b == NB - 1:
                    pe.wait_ge(state_ready, 2 * NB * STEPS)
                if b >= 2:
                    pe.wait_ge(o1_act, 2 * (b - 1))
                for o in range(2):
                    for f in range(FT):
                        last = mm(bank[2 * (b % 2) + o][:, :], wo[:, f, o * P:o * P + P],
                                  ST[:, f, b * BN:b * BN + BN], f == 0, f == 1)
                    last.then_inc(o1_ready, 1)

            def out2(b):
                pe.wait_ge(o1_act, 2 * (b + 1))
                if b == 0:
                    pe.wait_ge(gate_dve, 6 * NB * STEPS)
                if b >= 2:
                    pe.wait_ge(o2_dve, 2 * (b - 1))
                for q in range(BT):
                    for o in range(2):
                        last = mm(gate_bank[2 * (b % 2) + q // 2][:, (q % 2) * D:(q % 2) * D + D],
                                  TT[:, b % 2, o, q * P:q * P + P], wo[:, o, D:2 * D], o == 0, o == 1)
                    if q % 2 == 1:
                        last.then_inc(o2_ready, 1)

            out1(0)
            for b in range(NB):
                if b + 1 < NB:
                    out1(b + 1)
                out2(b)

        @block.scalar
        def _(act):
            def copy(o, i, scale=1.0, **kw):
                return nc.scalar.activation(o, i, ACT.Copy, scale=scale, **kw)

            act.dma_start(cst[:, :], consts).then_inc(ld_c, 16)
            act.dma_start(col[:, :], cols).then_inc(ld_c, 16)
            act.dma_start(raw["b_comb"][0:1, :], b_comb).then_inc(ld_c, 16)

            def convert(k, r):
                b, c, h = k // 8, k // 2 % 4, k % 2
                if r == 0:
                    act.wait_ge(ld_ring[k % RING], 16 * (k // RING + 1))
                if k == 16:
                    act.wait_ge(setup_done, 1)
                    act.wait_ge(st_fused, 16)
                t = BT * b + 2 * h + r
                copy(A[:, t, c * 512:c * 512 + 512], ring[:, k % RING, r, :],
                     accum_out=degA[:, t, c:c + 1]).then_inc(conv, 1)

            def move_adj(i):
                b, m = i // NT, i % NT
                act.wait_ge(tr_ready, i + 1)
                if i == NT:
                    act.wait_ge(hT_ready, NB)
                    act.wait_ge(h_lo, 4)
                if i == 3 * NT:
                    act.wait_ge(st_fused, 16)
                copy(AT[:, b, m, :], bank[3 + (i + 1) % 3][:, 0:256].bitcast(FP16),
                     accum_out=degT[:, m, b:b + 1]).then_inc(at_act, 1)

            for e in range(4):
                for part, (lo, hi) in enumerate(((0, 512), (512, GATES))):
                    act.wait_ge(fused_ready, 2 * e + part + 1)
                    copy(fusedS[:, e, lo:hi], bank[4 + 2 * (e % 2) + part][:, 0:hi - lo]).then_inc(fused_out, 1)
            act.wait_ge(var_ready, 1)
            nc.scalar.activation(nrm[:, 1, :], nrm[:, 0, :], ACT.Sqrt).then_inc(sqrt_ready, 1)
            for k in range(2):
                for r in range(2):
                    convert(k, r)
            for q in range(4):
                act.wait_ge(h_ready, q + 1)
                copy(hi_lo[:, BT * q:BT * q + BT, 0, :], h32[:, BT * q:BT * q + BT, :], SCALE).then_inc(h_hi, 1)

            def move_h(q):
                act.wait_ge(hT_ready, q + 1)
                copy(ST[:, 0, q * BN:q * BN + BN], bank[4 + 2 * (q % 2)][:, :]).then_inc(hT_act, 1)

            move_h(0)
            move_h(1)
            act.wait_ge(setup_done, 1)
            for w in range(2):
                copy(W12[:, 2 * w:2 * w + 2, :].rearrange("p k n -> p (k n)"), bank[w][:, :])
            copy(gcol[:, :, :].rearrange("p w t -> p (w t)"), bank[3][:, 0:12])
            copy(bias0, bank[2][:, 0:D]).then_inc(w12_out, 1)
            move_h(2)
            move_h(3)

            def block_end(b):
                def sums():
                    act.wait_ge(mask_used, NT * (b + 1))
                    if b > 0:
                        act.wait_ge(h2T_ready, b)
                        act.wait_ge(sn_lo, b)
                    copy(H[:, 0, :], bank[0][:, :], 1.0 / SCALE).then_inc(agg_act, 1)

                def root():
                    act.wait_ge(var_ready, b + 2)
                    nc.scalar.activation(nrm[:, 1, 0:BT], nrm[:, 0, 0:BT], ACT.Sqrt).then_inc(sqrt_ready, 1)

                def state():
                    act.wait_ge(h2_ready, b + 1)
                    act.wait_ge(st_x1, 16 * (b + 1))
                    copy(SN[:, BT * b:BT * b + BT, 0, :], h2, SCALE).then_inc(sn_hi, 1)

                def turned():
                    act.wait_ge(h2T_ready, b + 1)
                    copy(ST[:, 0, b * BN:b * BN + BN], bank[H2_BANKS[b]][:, :]).then_inc(s_act, 1)
                return sums, root, state, turned

            for i in range(NT * NB):
                k = 2 * (i // 4 + 1) + i % 4 // 2
                if k < 8 * NB:
                    convert(k, i % 2)
                if i % NT == 0 and i:
                    block_end(i // NT - 1)[0]()
                if i % 2 == 0:
                    move_adj(i)
                if i >= NT and i % NT in STAGE_AT:
                    block_end(i // NT - 1)[1 + STAGE_AT.index(i % NT)]()
            sums, root, state, turned = block_end(NB - 1)
            for stage in (sums, root, state, turned):
                stage()

            def out_pq(g):
                act.wait_ge(agg_done, g + 1)
                for f in range(FT):
                    copy(PQ[:, f, :], bank[f][:, :], 1.0 / SCALE).then_inc(pq_act, 1)

            def turn(s, e, banks):
                for j in range(2):
                    act.wait_ge(turn_ready, 8 * s + e + j + 1)
                    t = 2 * (e + j)
                    copy(SN[:, t:t + 2, 0, :], banks[j][:, :].rearrange("p (t d) -> p t d", t=2),
                         SCALE).then_inc(turn_hi, 1)

            def step(s, final):
                for b in range(NB):
                    g = NB * s + b
                    if b > 0:
                        act.wait_ge(state_ready, 2 * g)
                    out_pq(g)
                    for t in range(6):
                        act.wait_ge(gate_dve, 6 * g + t + 1)
                        v = (RS, Z, cand)[t // 2][:, t % 2, :]
                        nc.scalar.activation(v, v, ACT.Tanh if t >= 4 else ACT.Sigmoid,
                                             bias=col[:, 10 + t:11 + t]).then_inc(gate_act, 1)
                        if b == NB - 1 and not final and 1 <= t <= 3:
                            turn(s, 2 * (t - 1), (bank[0:2], bank[2:4])[(t - 1) % 2])
                if not final:
                    turn(s, 2 * (NB - 1), bank[6:8])

            with act.Fori(0, STEPS - 1) as s:
                step(s, False)
            step(STEPS - 1, True)
            for b in range(NB):
                for o in range(2):
                    act.wait_ge(o1_ready, 2 * b + o + 1)
                    if b >= 2:
                        act.wait_ge(o2_ready, 2 * (b - 1))
                    nc.scalar.activation(TT[:, b % 2, o, :], bank[2 * (b % 2) + o][:, :], ACT.Tanh,
                                         bias=col[:, 8 + o:9 + o]).then_inc(o1_act, 1)

        @block.vector
        def _(dve):
            v = nc.vector
            chain = [0]

            def link(ins):
                chain[0] += 1
                ins.then_inc(dve_chain, 1)
                dve.wait_ge(dve_chain, chain[0])

            def row_stats(tiles, base):
                for t in tiles:
                    if base == 0 and len(tiles) == NT and t % 8 == 0:
                        dve.wait_ge(ld_x[t // 8], 16)
                    ins = v.bn_stats(stat[:, t - base, :], xs[:, t, :])
                link(ins)

            def variance(tiles, base):
                for t in tiles:
                    ins = v.bn_aggr(mv[:, t - base, :], stat[:, t - base, :])
                link(ins)
                n = len(tiles)
                v.tensor_scalar(nrm[:, 0, 0:n], mv[:, 0:n, 1], EPS, None, ALU.add).then_inc(var_ready, 1)

            row_stats(range(NT), 0)
            variance(range(NT), 0)
            dve.wait_ge(ld_c, 48)
            link(v.tensor_copy(id16[:, :], cst[:, C_ID:C_ID + P]))
            v.tensor_copy(one16[:, :], cst[:, C_ONE:C_ONE + P]).then_inc(id16_ready, 1)
            for j in range(4):
                ins = v.tensor_scalar(L0[:, j, :], one_col, col[:, 4 + j:5 + j], None, ALU.mult)
            ins.then_inc(left_ready, 1)

            def newton(n, count):
                dve.wait_ge(sqrt_ready, count)
                ve, rt, sc, rs = (nrm[:, j, 0:n] for j in range(4))
                link(v.reciprocal(sc, rt))
                link(v.tensor_tensor(sc, sc, ve, ALU.mult))
                link(v.tensor_tensor(sc, sc, rt, ALU.add))
                link(v.tensor_scalar(sc, sc, 0.5, None, ALU.mult))
                link(v.reciprocal(rs, sc))

            newton(NT, 1)
            for q in range(4):
                for t in range(BT * q, BT * q + BT):
                    ins = v.tensor_scalar(h32[:, t, :], xs[:, t, :], mv[:, t, 0:1], nrm[:, 3, t:t + 1],
                                          ALU.subtract, ALU.mult)
                link(ins)
                hq = h32[:, BT * q:BT * q + BT, :].rearrange("p t d -> p (t d)")
                v.tensor_scalar(hq, hq, 0.0, None, ALU.max).then_inc(h_ready, 1)
            for q in range(4):
                dve.wait_ge(h_hi, q + 1)
                v.scalar_tensor_tensor(out=hi_lo[:, BT * q:BT * q + BT, 1, :], in0=h32[:, BT * q:BT * q + BT, :],
                                       scalar=SCALE, in1=hi_lo[:, BT * q:BT * q + BT, 0, :],
                                       op0=ALU.mult, op1=ALU.subtract).then_inc(h_lo, 1)
                dve.wait_ge(hT_ready, q + 1)
                v.tensor_copy(ST[:, 1, q * BN:q * BN + BN], bank[5 + 2 * (q % 2)][:, :]).then_inc(hT_dve, 1)

            def move_adj(i):
                b, m = i // NT, i % NT
                dve.wait_ge(tr_ready, i + 1)
                if i == 3 * NT + 1:
                    dve.wait_ge(st_fused, 16)
                v.tensor_scalar(AT[:, b, m, :], bank[3 + (i + 1) % 3][:, 0:256].bitcast(FP16), 1.0, None, ALU.mult,
                                ALU.add, accum_out=degT[:, m, b:b + 1]).then_inc(at_dve, 1)

            def make_mask(i):
                b, m = i // NT, i % NT
                if i % 2 == 0:
                    dve.wait_ge(at_act, i // 2 + 1)
                else:
                    dve.wait_ge(at_dve, i // 2 + 1)
                if i >= 4:
                    dve.wait_ge(mask_used, i - 3)
                v.tensor_scalar(mask[:, i % 4, :], AT[:, b, m, :], 0.0, None, ALU.is_gt).then_inc(mask_ready, 1)

            def sums(b):
                dve.wait_ge(mask_used, NT * (b + 1))
                if b > 0:
                    dve.wait_ge(h2T_ready, b)
                    dve.wait_ge(sn_hi, b)
                v.tensor_scalar(H[:, 1, :], bank[1][:, :], 1.0 / SCALE, None, ALU.mult).then_inc(agg_dve, 1)
                tiles = slice(BT * b, BT * b + BT)
                v.tensor_scalar(rdeg[:, tiles], bank[2][:, tiles], 1.0, None, ALU.max).then_inc(rdeg_ready, 1)
                dve.wait_ge(rdeg_ready, b + 1)
                link(v.reciprocal(rdeg[:, tiles], rdeg[:, tiles]))

            def residual(b, half):
                for q in (2 * half, 2 * half + 1):
                    t = BT * b + q
                    o = bank[6 + q % 2]
                    u = u_tmp[:, :]
                    dve.wait_ge(dense_ready, t + 1)
                    link(v.scalar_tensor_tensor(out=u, in0=o[:, D:2 * D], scalar=rdeg[:, t:t + 1], in1=bias0,
                                                op0=ALU.mult, op1=ALU.add))
                    link(v.tensor_tensor(u, u, o[:, 0:D], ALU.add))
                    v.scalar_tensor_tensor(out=xs[:, t, :], in0=u, scalar=0.0, in1=xs[:, t, :],
                                           op0=ALU.max, op1=ALU.add).then_inc(x1_ready, 1)
                    dve.wait_ge(x1_ready, t + 1)

            def normed(b):
                dve.wait_ge(dense_ready, BT * (b + 1))
                for q in range(BT):
                    ins = v.tensor_scalar(h2[:, q, :], xs[:, BT * b + q, :], mv[:, q, 0:1], nrm[:, 3, q:q + 1],
                                          ALU.subtract, ALU.mult)
                link(ins)
                v.tensor_scalar(Hf, Hf, 0.0, None, ALU.max).then_inc(h2_ready, 1)

            def state(b):
                dve.wait_ge(sn_hi, b + 1)
                tiles = slice(BT * b, BT * b + BT)
                v.scalar_tensor_tensor(out=SN[:, tiles, 1, :], in0=h2, scalar=SCALE, in1=SN[:, tiles, 0, :],
                                       op0=ALU.mult, op1=ALU.subtract).then_inc(sn_lo, 1)

            def turned(b):
                dve.wait_ge(h2T_ready, b + 1)
                v.tensor_copy(ST[:, 1, b * BN:b * BN + BN], bank[H2_BANKS[b] + 1][:, :]).then_inc(s_dve, 1)

            for i in range(NT * NB + 1):
                if i:
                    make_mask(i - 1)
                if i % NT == 0 and i:
                    sums(i // NT - 1)
                if i % 2 == 1:
                    move_adj(i)
                if i > NT and i % NT in (2, 4):
                    residual(i // NT - 1, i % NT // 4)
                b = i // NT - 1
                if i > NT and i % NT in (5, 6):
                    row_stats(range(BT * b + 2 * (i % NT - 5), BT * b + 2 * (i % NT - 4)), BT * b)
                if i > NT and i % NT == 7:
                    variance(range(BT * b, BT * b + BT), BT * b)
                if i > NT and i % NT == STAGE_AT[0] + 1:
                    newton(BT, b + 2)
                if i > NT and i % NT == STAGE_AT[0] + 2:
                    normed(b)
                if i > NT and i % NT == STAGE_AT[1] + 1:
                    state(i // NT - 1)
                if i > NT and i % NT == STAGE_AT[2] + 1:
                    turned(i // NT - 1)
            for half in range(2):
                residual(NB - 1, half)
            dve.wait_ge(conv, 4 * NT)
            dve.wait_ge(at_act, NT * NB // 2)
            v.tensor_reduce(degs[:, 0, :], degA[:, :, :], mybir.AxisListType.X, ALU.add)
            v.tensor_reduce(degs[:, 1, :], degT[:, :, :], mybir.AxisListType.X, ALU.add)
            row_stats(range(BT * (NB - 1), NT), BT * (NB - 1))
            variance(range(BT * (NB - 1), NT), BT * (NB - 1))
            for w in range(2):
                for t in range(NT):
                    ins = v.tensor_scalar(diag[:, w, t, :], id16[:, :], degs[:, w, t:t + 1], None, ALU.mult)
            ins.then_inc(diag_ready, 1)
            newton(BT, NB + 1)
            normed(NB - 1)

            def out_degrees(w, dst):
                for b in range(NB):
                    dve.wait_ge(deg_ready, NB * w + b + 1)
                    v.tensor_copy(dst[:, b * BN:b * BN + BN], gate_bank[b][:, :]).then_inc(deg_out, 1)

            out_degrees(0, degA_all)
            state(NB - 1)
            turned(NB - 1)
            dve.wait_ge(h2T_ready, NB)
            out_degrees(1, degT_all)
            dve.wait_ge(deg_out, 2 * NB)

            def out_pq(g):
                dve.wait_ge(agg_done, g + 1)
                for f in range(FT):
                    v.tensor_scalar(PQ[:, 2 + f, :], bank[2 + f][:, :], 1.0 / SCALE, None,
                                    ALU.mult).then_inc(pq_dve, 1)

            def turn(s, e, banks):
                for j in range(2):
                    dve.wait_ge(turn_hi, 8 * s + e + j + 1)
                    t = 2 * (e + j)
                    v.scalar_tensor_tensor(out=SN[:, t:t + 2, 1, :],
                                           in0=banks[j][:, :].rearrange("p (t d) -> p t d", t=2),
                                           scalar=SCALE, in1=SN[:, t:t + 2, 0, :],
                                           op0=ALU.mult, op1=ALU.subtract).then_inc(turn_lo, 1)

            base = chain[0]
            PER_BLOCK = 10

            def step(s, final):
                for b in range(NB):
                    g = NB * s + b
                    nodes = slice(b * BN, b * BN + BN)
                    c = base + PER_BLOCK * g

                    def add_bias(t):
                        o = (RS, Z, cand)[t // 2][:, t % 2, :]
                        dve.wait_ge(gate_ready, 6 * g + t + 1)
                        v.scalar_tensor_tensor(out=o, in0=degA_all[:, nodes], scalar=gcol[:, 0, t:t + 1],
                                               in1=gate_bank[t % 4][:, :], op0=ALU.mult,
                                               op1=ALU.add).then_inc(dve_chain, 1)
                        dve.wait_ge(dve_chain, c + t + 1)
                        v.scalar_tensor_tensor(out=o, in0=degT_all[:, nodes], scalar=gcol[:, 1, t:t + 1],
                                               in1=o, op0=ALU.mult, op1=ALU.add).then_inc(gate_dve, 1)

                    out_pq(g)
                    add_bias(0)
                    add_bias(1)
                    for f in range(FT):
                        dve.wait_ge(gate_act, 6 * g + f + 1)
                        v.tensor_tensor(RS[:, f, :], RS[:, f, :], ST[:, f, nodes], ALU.mult).then_inc(rs_ready, 1)
                    for t in (2, 3):
                        if b == NB - 1 and not final:
                            turn(s, 2 * (t - 2), (bank[0:2], bank[2:4])[t - 2])
                        add_bias(t)
                    if b == NB - 1 and not final:
                        turn(s, 4, bank[0:2])
                    add_bias(4)
                    add_bias(5)
                    for f in range(FT):
                        new = cand[:, f, :]
                        dve.wait_ge(gate_act, 6 * g + 5 + f)
                        v.tensor_tensor(new, new, ST[:, f, nodes], ALU.subtract).then_inc(dve_chain, 1)
                        dve.wait_ge(dve_chain, c + 6 + 2 * f + 1)
                        v.tensor_tensor(new, new, Z[:, f, :], ALU.mult).then_inc(dve_chain, 1)
                        dve.wait_ge(dve_chain, c + 6 + 2 * f + 2)
                        v.tensor_tensor(ST[:, f, nodes], ST[:, f, nodes], new, ALU.add).then_inc(state_ready, 1)
                if not final:
                    turn(s, 2 * (NB - 1), bank[6:8])

            with dve.Fori(0, STEPS - 1) as s:
                step(s, False)
            step(STEPS - 1, True)
            dve.wait_ge(ld_o, 48)
            for t in range(NT):
                ins = v.tensor_tensor(x1o[:, t, :], x1o[:, t, :], ob, ALU.add)
            ins.then_inc(dve_chain, 1)
            dve.wait_ge(dve_chain, base + PER_BLOCK * NB * STEPS + 1)
            for e in range(2 * NB):
                dve.wait_ge(o2_ready, e + 1)
                tiles = slice(2 * e, 2 * e + 2)
                v.tensor_tensor(res[:, tiles, :].rearrange("p t d -> p (t d)"),
                                gate_bank[e % 4][:, :],
                                x1o[:, tiles, :].rearrange("p t d -> p (t d)"), ALU.add).then_inc(o2_dve, 1)


def kernel(**inputs):
    import numpy as np
    import concourse.bacc as bacc
    from concourse.bass_utils import run_bass_kernel_spmd

    a = {k: np.asarray(v) for k, v in inputs.items()}
    f = np.float32
    consts = np.zeros((P, C_END), f)
    consts[:, C_ID:C_ID + P] = np.eye(P, dtype=f)
    consts[:, C_ONE:C_ONE + P] = 1.0
    two = lambda v: v.reshape(2, P).T
    arrays = {
        "x": a["x"], "adj": a["adj"],
        "w_in": a["L1_gnn_in_W"], "w_out": a["L1_gnn_out_W"],
        "wg_t": np.concatenate([a["L1_gnn_r_W"].T, a["L1_gnn_z_W"].T, a["L1_gnn_h_W"].T], 1),
        "w0_t": np.concatenate([a["L0_gnn_W_self"].T, a["L0_gnn_W_nb"].T], 1),
        "w_comb": a["L0_gnn_W_comb"],
        "w_o": np.concatenate([a["L1_gnn_o1_W"].T, a["L1_gnn_o2_W"].T], 1),
        "cols": np.concatenate([two(a["L1_gnn_in_b"]), two(a["L1_gnn_out_b"]), two(a["L0_gnn_b_self"]),
                                two(a["L0_gnn_b_nb"]), two(a["L1_gnn_o1_b"])]
                               + [two(a[f"L1_gnn_{g}_b"]) for g in "rzh"], 1),
        "b_comb": a["L0_gnn_b_comb"][None],
        "o2_b": a["L1_gnn_o2_b"],
        "consts": consts,
    }
    arrays = {k: np.ascontiguousarray(v) for k, v in arrays.items()}
    nc = bacc.Bacc("TRN2", target_bir_lowering=False, num_devices=1)
    args = [nc.dram_tensor(f"in_{k}", v.shape, mybir.dt.from_np(v.dtype), kind="ExternalInput").ap()
            for k, v in arrays.items()]
    out = nc.dram_tensor("out", (N, D), FP32, kind="ExternalOutput").ap()
    graph_net(nc, *args, out)
    r = run_bass_kernel_spmd(nc, [{f"in_{k}": v for k, v in arrays.items()}], core_ids=[0])
    return r.results[0]["out"]
```
